# Optimizing a Trainium2 kernel written in Bass

```python
import numpy as np
import jax
import jax.numpy as jnp

def _softmax(x, axis=-1):
    return jax.nn.softmax(x, axis=axis)

def _gelu(x):
    return jax.nn.gelu(x, approximate=True)

def _silu(x):
    return jax.nn.silu(x)

def _sigmoid(x):
    return jax.nn.sigmoid(x)

def _layernorm(x, axis=-1, eps=1e-05):
    m = jnp.mean(x, axis=axis, keepdims=True)
    v = jnp.var(x, axis=axis, keepdims=True)
    return (x - m) / jnp.sqrt(v + eps)

def _scatter_add(tgt, idx, src, axis=0):
    return tgt.at[idx].add(src)

def _segment_sum(src, seg, n):
    return jax.ops.segment_sum(src, seg, n)
kernel_name = 'mk_xattn_seq_d1_seqx_r4_bf79f8'

def setup_inputs(seed: int=0):
    np.random.seed(seed)
    _w = jnp.asarray

    def _rec_inputs():
        import jax
        import jax.numpy as jnp
        _rk = jax.random.key(seed)
        x = -0.000125 + 0.9999 * jax.random.normal(jax.random.fold_in(_rk, 1), (32, 112, 512), jnp.float32)
        _lenS = 112 - jax.random.randint(jax.random.fold_in(_rk, 7), (32,), 0, max(1, 112 // 4) + 1, jnp.int32)
        _lenS2 = 375 - jax.random.randint(jax.random.fold_in(_rk, 8), (32,), 0, max(1, 375 // 4) + 1, jnp.int32)
        _ctx_1024P = jax.random.normal(jax.random.fold_in(_rk, 11), (32, 16, 256), jnp.float32)
        _ctx_1024c = jax.random.dirichlet(jax.random.fold_in(_rk, 511), 0.3 * jnp.ones((16,), jnp.float32), (32, 375))
        _ctx_1024t = jnp.einsum('bsk,bkd->bsd', _ctx_1024c, _ctx_1024P)
        _ctx_1024t = _ctx_1024t * jax.lax.rsqrt(jnp.mean(jnp.square(_ctx_1024t)) + 1e-12) * 0.953939
        ctx_1024 = 4.13588e-05 + 0.999923 * (_ctx_1024t + 0.3 * jax.random.normal(jax.random.fold_in(_rk, 611), (32, 375, 256), jnp.float32))
        return (x, ctx_1024)
    x, ctx_1024 = _rec_inputs()

    def _L0_xattn_setup():
        import jax, jax.numpy as jnp
        import numpy as np
        EPS = 1e-06

        def _rmsnorm(x, w):
            var = jnp.mean(jnp.square(x), axis=-1, keepdims=True)
            return x * jax.lax.rsqrt(var + EPS) * w
        key = jax.random.key(seed)
        ks = jax.random.split(key, 6)
        B, N, M = (4, 1024, 512)
        d_model, memory_dim = (512, 256)
        hidden_states = jax.random.normal(ks[0], (B, N, d_model), dtype=jnp.float32)
        memory = jax.random.normal(ks[1], (B, M, memory_dim), dtype=jnp.float32)
        W_mem = jax.random.normal(ks[2], (d_model, memory_dim), dtype=jnp.float32) / np.sqrt(memory_dim)
        W_gate = jax.random.normal(ks[3], (d_model, 2 * d_model), dtype=jnp.float32) / np.sqrt(2 * d_model)
        b_gate = jax.random.normal(ks[4], (d_model,), dtype=jnp.float32) * 0.01
        norm_w = jnp.ones((d_model,), dtype=jnp.float32)
        return {'hidden_states': hidden_states, 'memory': memory, 'W_mem': W_mem, 'W_gate': W_gate, 'b_gate': b_gate, 'norm_w': norm_w}
    _L0_xattn_all = _L0_xattn_setup()
    _L0_xattn_in = {k: v for k, v in _L0_xattn_all.items() if k in ('W_mem', 'W_gate', 'b_gate', 'norm_w')}
    del _L0_xattn_all
    return {'x': x, 'ctx_1024': ctx_1024, 'L0_xattn_W_mem': _L0_xattn_in['W_mem'], 'L0_xattn_W_gate': _L0_xattn_in['W_gate'], 'L0_xattn_b_gate': _L0_xattn_in['b_gate'], 'L0_xattn_norm_w': _L0_xattn_in['norm_w']}

def reference(x, ctx_1024, L0_xattn_W_mem, L0_xattn_W_gate, L0_xattn_b_gate, L0_xattn_norm_w):
    import jax
    import jax.numpy as jnp

    def _L0_xattn_ref(hidden_states, memory, W_mem, W_gate, b_gate, norm_w):
        import jax, jax.numpy as jnp
        import numpy as np
        EPS = 1e-06

        def _rmsnorm(x, w):
            var = jnp.mean(jnp.square(x), axis=-1, keepdims=True)
            return x * jax.lax.rsqrt(var + EPS) * w
        D = hidden_states.shape[-1]
        memory_proj = jnp.einsum('bme,de->bmd', memory, W_mem)
        scores = jnp.einsum('bnd,bmd->bnm', hidden_states, memory_proj) / jnp.sqrt(jnp.float32(D))
        attn = jax.nn.softmax(scores, axis=-1)
        memory_context = jnp.einsum('bnm,bmd->bnd', attn, memory_proj)
        gate_input = jnp.concatenate([hidden_states, memory_context], axis=-1)
        gate = jax.nn.sigmoid(jnp.einsum('bnf,df->bnd', gate_input, W_gate) + b_gate)
        fused = hidden_states + gate * memory_context
        return _rmsnorm(fused, norm_w)
    x = _L0_xattn_ref(x, ctx_1024, L0_xattn_W_mem, L0_xattn_W_gate, L0_xattn_b_gate, L0_xattn_norm_w)
    return x

_drawn_inputs = setup_inputs


def setup_inputs(seed=0):
    import zlib

    import numpy as np

    out = dict(_drawn_inputs(seed))
    spreads = {'L0_xattn_norm_w': (1.0, 0.2)}
    factors = {'L0_xattn_b_gate': 50.561}
    for name, (base, spread) in spreads.items():
        noise = np.random.default_rng([zlib.crc32(name.encode()), seed]).standard_normal(out[name].shape)
        drawn = base * np.exp(spread * noise) if base else spread * noise
        out[name] = jnp.asarray(drawn.astype(out[name].dtype))
    for name, factor in factors.items():
        out[name] = (out[name] * factor).astype(out[name].dtype)
    return out
```

```python
from contextlib import ExitStack

import concourse.bass as bass
from concourse import mybir

F32 = mybir.dt.float32
F32R = mybir.dt.float32r
ACT = mybir.ActivationFunctionType
ALU = mybir.AluOpType
AX = mybir.AxisListType

P = 128
BATCHES, ROWS, D = 32, 112, 512
KEYS, E = 375, 256
EPS = 1e-6

GROUP = 8
GROUPS = BATCHES // GROUP
COLS = GROUP * ROWS
TILES = COLS // P
DC, EC = D // P, E // P
KC = -(-KEYS // P)
KPAD = KC * P
KEVEN = KEYS + KEYS % 2
UNITS = [(0, 256), (256, 320), (576, 320)]
PIECES = len(UNITS) * EC
X_SLOTS = 4


def unit_of(batch):
    end = (batch + 1) * ROWS
    return next(u for u, (c, n) in enumerate(UNITS) if end <= c + n)


def x_slot_use(g, t):
    slot = t % X_SLOTS
    a_group = len(range(slot, TILES, X_SLOTS))
    return a_group * g + t // X_SLOTS + 1


def y_slot_use(g, t):
    a_group = len(range(t % 2, TILES, 2))
    return a_group * g + t // 2


def build_gated_cross_attention(nc, x_d, xT_d, mem_d, memT_d, wm_d, wmT_d, wgT_d, b_d, nw_d, out_d):
    ctx = ExitStack()
    with ctx:
        def sb(name, shape, dt=F32):
            return ctx.enter_context(nc.sbuf_tensor(name, shape, dt))

        def pb(name, shape):
            return ctx.enter_context(nc.psum_tensor(name, shape, F32))

        def sem(name):
            return ctx.enter_context(nc.semaphore(name))

        ident = sb("ident", [P, P])
        wm_raw = sb("wm_raw", [P, DC, E])
        wm_hi, wm_lo = (sb(f"wm_{s}", [P, DC, E], F32R) for s in ("hi", "lo"))
        wmT_hi, wmT_lo = (sb(f"wmT_{s}", [P, EC, D], F32R) for s in ("hi", "lo"))
        wgx_hi, wgx_lo = (sb(f"wgx_{s}", [P, DC, D], F32R) for s in ("hi", "lo"))
        wga_hi, wga_lo = (sb(f"wga_{s}", [P, EC, D], F32R) for s in ("hi", "lo"))
        b_gate = sb("b_gate", [P, D])
        norm_w = sb("norm_w", [P, D])
        xT_raw = sb("xT_raw", [P, DC, COLS])
        xT_hi, xT_lo = (sb(f"xT_{s}", [P, DC, COLS], F32R) for s in ("hi", "lo"))
        qT_hi, qT_lo = (sb(f"qT_{s}", [P, EC, COLS], F32R) for s in ("hi", "lo"))
        amT_hi, amT_lo = (sb(f"amT_{s}", [P, EC, COLS], F32R) for s in ("hi", "lo"))
        memT_raw = sb("memT_raw", [P, 2, EC, KEVEN])
        memT_hi, memT_lo = (sb(f"memT_{s}", [P, 2, EC, KEVEN], F32R) for s in ("hi", "lo"))
        mem_raw = sb("mem_raw", [P, 2, KC, E])
        mem_hi, mem_lo = (sb(f"mem_{s}", [P, 2, KC, E], F32R) for s in ("hi", "lo"))
        probs = sb("probs", [ROWS, 2, KPAD])
        pT_hi, pT_lo = (sb(f"pT_{s}", [P, 2, KC, ROWS], F32R) for s in ("hi", "lo"))
        am = sb("am", [ROWS, E])
        x_rows = sb("x_rows", [P, X_SLOTS, D])
        work = sb("work", [P, 8, D])
        z, h, y = work[:, 0:2], work[:, 2:4], work[:, 4:6]
        u, squares = work[:, 6], work[:, 7]
        top = sb("top", [ROWS, 2])
        shift = sb("shift", [ROWS, 2])
        total = sb("total", [ROWS, 2])
        share = sb("share", [ROWS, 2])
        meansq = sb("meansq", [P, 2])
        guarded = sb("guarded", [P, 2])
        rstd = sb("rstd", [P, 2])
        minus_half = sb("minus_half", [P, 1])
        eps = sb("eps", [P, 1])
        wga_raw = work[:, 0:DC]
        wmT_raw = work[:, DC:DC + EC]
        wgx_raw = x_rows

        q_ps = [pb(f"q_ps{i}", [P, D]) for i in range(2)]
        score_ps = pb("score_ps", [P, D])
        pT_ps = pb("pT_ps", [P, D])
        am_bank = pb("am_bank", [P, D])
        ctx_ps = pb("ctx_ps", [P, D])
        gate_ps = [pb(f"gate_ps{i}", [P, D]) for i in range(2)]
        scores = score_ps[0:ROWS, 0:KEVEN]
        probsT = pT_ps[:, 0:KC * ROWS].rearrange("p (c n) -> p c n", c=KC)
        am_ps = am_bank[0:ROWS, 0:E]
        amT_ps = am_bank[:, E:E + EC * ROWS].rearrange("p (c n) -> p c n", c=EC)

        wm_loaded, wga_loaded, wgx_loaded, wmT_loaded, vectors_loaded = map(
            sem, ("wm_loaded", "wga_loaded", "wgx_loaded", "wmT_loaded", "vectors_loaded"))
        wm_hi_ready, wm_lo_ready = sem("wm_hi_ready"), sem("wm_lo_ready")
        wgx_hi_ready, wgx_lo_ready = sem("wgx_hi_ready"), sem("wgx_lo_ready")
        wmT_hi_ready, wmT_lo_ready = sem("wmT_hi_ready"), sem("wmT_lo_ready")
        wga_done, wga_hi_ready, wga_lo_ready = sem("wga_done"), sem("wga_hi_ready"), sem("wga_lo_ready")
        blank_ready, ident_ready, padding_ready = sem("blank_ready"), sem("ident_ready"), sem("padding_ready")
        constants_ready = sem("constants_ready")
        xT_loaded = [sem(f"xT_loaded{i}") for i in range(len(UNITS))]
        memT_loaded = [sem(f"memT_loaded{i}") for i in range(2)]
        mem_loaded = [sem(f"mem_loaded{i}") for i in range(2)]
        x_loaded = [sem(f"x_loaded{i}") for i in range(X_SLOTS)]
        y_stored = [sem(f"y_stored{i}") for i in range(2)]
        xT_hi_ready, xT_lo_ready = sem("xT_hi_ready"), sem("xT_lo_ready")
        memT_hi_ready, memT_lo_ready = sem("memT_hi_ready"), sem("memT_lo_ready")
        mem_hi_ready, mem_lo_ready = sem("mem_hi_ready"), sem("mem_lo_ready")
        q_done, q_hi_ready, q_lo_ready = sem("q_done"), sem("q_hi_ready"), sem("q_lo_ready")
        scores_done, top_ready, shift_ready = sem("scores_done"), sem("top_ready"), sem("shift_ready")
        probs_ready, share_ready = sem("probs_ready"), sem("share_ready")
        pT_done, pT_hi_ready, pT_lo_ready = sem("pT_done"), sem("pT_hi_ready"), sem("pT_lo_ready")
        am_done, am_ready = sem("am_done"), sem("am_ready")
        amT_done, amT_hi_ready, amT_lo_ready = sem("amT_done"), sem("amT_hi_ready"), sem("amT_lo_ready")
        gate_x_done, gate_done, ctx_done = sem("gate_x_done"), sem("gate_done"), sem("ctx_done")
        z_ready, tanh_ready, u_ready, h_ready = sem("z_ready"), sem("tanh_ready"), sem("u_ready"), sem("h_ready")
        meansq_ready, guarded_ready, rstd_ready = sem("meansq_ready"), sem("guarded_ready"), sem("rstd_ready")
        y_ready = sem("y_ready")

        block = ctx.enter_context(nc.Block())

        @block.sync
        def _(sp):
            def load_xT(g, unit):
                c, n = UNITS[unit]
                sp.dma_start(xT_raw[:, :, c:c + n], xT_d[g, :, :, c:c + n]).then_inc(xT_loaded[unit], 16)

            def load_memory(batch, slot):
                sp.dma_start(memT_raw[:, slot], memT_d[batch]).then_inc(memT_loaded[slot], 16)
                sp.dma_start(mem_raw[:, slot], mem_d[batch]).then_inc(mem_loaded[slot], 16)

            def load_x(tile, slot):
                sp.dma_start(x_rows[:, slot], x_d[tile]).then_inc(x_loaded[slot], 16)

            sp.dma_start(wm_raw[:], wm_d).then_inc(wm_loaded, 16)
            load_xT(0, 0)
            sp.dma_start(wga_raw, wgT_d[:, DC:2 * DC]).then_inc(wga_loaded, 16)
            load_memory(0, 0)
            load_xT(0, 1)
            sp.dma_start(wgx_raw[:], wgT_d[:, 0:DC]).then_inc(wgx_loaded, 16)
            sp.dma_start(wmT_raw, wmT_d).then_inc(wmT_loaded, 16)
            load_xT(0, 2)
            load_memory(1, 1)
            sp.dma_start(b_gate[:], b_d.partition_broadcast(P)).then_inc(vectors_loaded, 16)
            sp.dma_start(norm_w[:], nw_d.partition_broadcast(P)).then_inc(vectors_loaded, 16)
            for slot in range(2):
                sp.sem_inc(y_stored[slot], 16)
            sp.wait_ge(wgx_hi_ready, 1)
            sp.wait_ge(wgx_lo_ready, 1)
            for t in range(X_SLOTS):
                load_x(t, t)

            def finish(g, t, last):
                sp.wait_ge(h_ready, TILES * g + t + 1)
                if t + X_SLOTS < TILES:
                    load_x(TILES * g + t + X_SLOTS, t % X_SLOTS)
                elif not last:
                    load_x(TILES * (g + 1) + t % X_SLOTS, t % X_SLOTS)
                sp.wait_ge(y_ready, TILES * g + t + 1)
                sp.dma_start(out_d[TILES * g + t], y[:, t % 2]).then_inc(y_stored[t % 2], 16)

            def group(g, last):
                for b in range(GROUP):
                    if not last or b + 2 < GROUP:
                        sp.wait_ge(memT_lo_ready, GROUP * g + b + 1)
                        sp.wait_ge(mem_lo_ready, GROUP * g + b + 1)
                        load_memory(GROUP * g + b + 2, b % 2)
                    if not last and b in (1, 3, 5):
                        unit = b // 2
                        sp.wait_ge(xT_lo_ready, len(UNITS) * g + unit + 1)
                        load_xT(g + 1, unit)
                    if b >= 3:
                        finish(g, b - 3, last)
                finish(g, TILES - 2, last)
                finish(g, TILES - 1, last)

            with sp.Fori(0, GROUPS - 1) as g:
                group(g, False)
            group(GROUPS - 1, True)
            for slot in range(2):
                sp.wait_ge(y_stored[slot], 16 * (1 + y_slot_use(GROUPS, slot)))

        @block.tensor
        def _(pe):
            def product(out, lefts, rights, first=True, last=True):
                n = 3 * len(lefts)
                i = 0
                for (l_hi, l_lo), (r_hi, r_lo) in zip(lefts, rights):
                    for left, right in ((l_hi, r_hi), (l_hi, r_lo), (l_lo, r_hi)):
                        mm = pe.matmul(out, left, right, start=first and i == 0, stop=last and i == n - 1)
                        i += 1
                return mm

            pe.wait_ge(wm_loaded, 16)
            pe.wait_ge(wga_loaded, 16)
            for c in range(EC):
                for i in range(DC):
                    mm = pe.matmul(q_ps[c][:], wm_raw[:, i, c * P:(c + 1) * P], wga_raw[:, i],
                                   start=i == 0, stop=i == DC - 1)
                mm.then_inc(wga_done, 1)
            pe.wait_ge(ident_ready, 1)
            pe.wait_ge(wm_hi_ready, 1)
            pe.wait_ge(wm_lo_ready, 1)
            pe.wait_ge(wga_lo_ready, EC)

            WHOLE, OPEN, CLOSE = (True, True), (True, False), (False, True)

            def chunks_of(part, n):
                first, last = part
                return range(0 if first else n // 2, n if last else n // 2)

            def q_piece(g, unit, half, part=WHOLE):
                n = EC * unit + half
                if half == 0 and part[0]:
                    pe.wait_ge(xT_hi_ready, len(UNITS) * g + unit + 1)
                    pe.wait_ge(xT_lo_ready, len(UNITS) * g + unit + 1)
                if n >= 2 and part[0]:
                    pe.wait_ge(q_lo_ready, PIECES * g + n - 1)
                c, w = UNITS[unit]
                es = slice(half * P, (half + 1) * P)
                mm = product(q_ps[n % 2][:, 0:w],
                             [(wm_hi[:, i, es], wm_lo[:, i, es]) for i in chunks_of(part, DC)],
                             [(xT_hi[:, i, c:c + w], xT_lo[:, i, c:c + w]) for i in chunks_of(part, DC)], *part)
                if part[1]:
                    mm.then_inc(q_done, 1)

            def score(g, b):
                pe.wait_ge(q_lo_ready, PIECES * g + EC * (unit_of(b) + 1))
                pe.wait_ge(memT_hi_ready, GROUP * g + b + 1)
                pe.wait_ge(memT_lo_ready, GROUP * g + b + 1)
                cols = slice(b * ROWS, (b + 1) * ROWS)
                product(scores,
                        [(qT_hi[:, c, cols], qT_lo[:, c, cols]) for c in range(EC)],
                        [(memT_hi[:, b % 2, c], memT_lo[:, b % 2, c]) for c in range(EC)]).then_inc(scores_done, 1)

            def probs_turn(g, b):
                pe.wait_ge(probs_ready, GROUP * g + b + 1)
                for c in range(KC):
                    mm = pe.transpose(probsT[:, c], probs[:, b % 2, c * P:(c + 1) * P], ident[0:ROWS, 0:ROWS])
                mm.then_inc(pT_done, 1)

            def attend(g, b):
                pe.wait_ge(pT_lo_ready, GROUP * g + b + 1)
                pe.wait_ge(mem_hi_ready, GROUP * g + b + 1)
                pe.wait_ge(mem_lo_ready, GROUP * g + b + 1)
                if b > 0:
                    pe.wait_ge(amT_lo_ready, GROUP * g + b)
                product(am_ps,
                        [(pT_hi[:, b % 2, c], pT_lo[:, b % 2, c]) for c in range(KC)],
                        [(mem_hi[:, b % 2, c], mem_lo[:, b % 2, c]) for c in range(KC)]).then_inc(am_done, 1)

            def am_turn(g, b):
                pe.wait_ge(am_ready, GROUP * g + b + 1)
                for c in range(EC):
                    mm = pe.transpose(amT_ps[:, c], am[:, c * P:(c + 1) * P], ident[0:ROWS, 0:ROWS])
                mm.then_inc(amT_done, 1)

            def gate_x(g, t):
                pe.wait_ge(wgx_hi_ready, 1)
                pe.wait_ge(wgx_lo_ready, 1)
                if t >= 2:
                    pe.wait_ge(z_ready, TILES * g + t - 1)
                cols = slice(t * P, (t + 1) * P)
                product(gate_ps[t % 2][:],
                        [(xT_hi[:, i, cols], xT_lo[:, i, cols]) for i in range(DC)],
                        [(wgx_hi[:, i], wgx_lo[:, i]) for i in range(DC)], last=False).then_inc(gate_x_done, 1)

            def am_columns(t, part=WHOLE):
                cols = slice(t * P, (t + 1) * P)
                return [(amT_hi[:, c, cols], amT_lo[:, c, cols]) for c in chunks_of(part, EC)]

            def gate_am(g, t):
                pe.wait_ge(wga_lo_ready, EC)
                pe.wait_ge(amT_lo_ready, GROUP * g + t + 2)
                product(gate_ps[t % 2][:], am_columns(t),
                        [(wga_hi[:, c], wga_lo[:, c]) for c in range(EC)], first=False).then_inc(gate_done, 1)

            def context(g, t, part=WHOLE):
                pe.wait_ge(wmT_hi_ready, 1)
                pe.wait_ge(wmT_lo_ready, 1)
                if t > 0 and part[0]:
                    pe.wait_ge(u_ready, TILES * g + t)
                mm = product(ctx_ps[:], am_columns(t, part),
                             [(wmT_hi[:, c], wmT_lo[:, c]) for c in chunks_of(part, EC)], *part)
                if part[1]:
                    mm.then_inc(ctx_done, 1)

            def group(g):
                q_piece(g, 0, 0)
                q_piece(g, 0, 1)
                q_piece(g, 1, 0)
                for b in range(GROUP):
                    score(g, b)
                    if b == 0:
                        q_piece(g, 1, 1)
                    else:
                        gate_x(g, b - 1)
                    probs_turn(g, b)
                    if b < 2:
                        q_piece(g, 2, b, OPEN)
                    else:
                        gate_am(g, b - 2)
                    attend(g, b)
                    if b < 2:
                        q_piece(g, 2, b, CLOSE)
                    else:
                        context(g, b - 2, OPEN if b == GROUP - 1 else WHOLE)
                    am_turn(g, b)
                context(g, TILES - 2, CLOSE)
                gate_am(g, TILES - 1)
                context(g, TILES - 1)

            with pe.Fori(0, GROUPS - 1) as g:
                group(g)
            group(GROUPS - 1)

        @block.scalar
        def _(act):
            def high(out, in_):
                return act.activation(out, in_, ACT.Copy)

            def split_xT(g, unit):
                c, n = UNITS[unit]
                act.wait_ge(xT_loaded[unit], 16 * (g + 1))
                high(xT_hi[:, :, c:c + n], xT_raw[:, :, c:c + n]).then_inc(xT_hi_ready, 1)

            def split_memT(g, b):
                act.wait_ge(memT_loaded[b % 2], 16 * (GROUP // 2 * g + b // 2 + 1))
                high(memT_hi[:, b % 2], memT_raw[:, b % 2]).then_inc(memT_hi_ready, 1)

            def split_mem(g, b):
                act.wait_ge(mem_loaded[b % 2], 16 * (GROUP // 2 * g + b // 2 + 1))
                high(mem_hi[:, b % 2], mem_raw[:, b % 2]).then_inc(mem_hi_ready, 1)

            def q_high(g, unit, half):
                c, w = UNITS[unit]
                n = EC * unit + half
                act.wait_ge(q_done, PIECES * g + n + 1)
                high(qT_hi[:, half, c:c + w], q_ps[n % 2][:, 0:w]).then_inc(q_hi_ready, 1)

            def exponentials(g, b):
                act.wait_ge(shift_ready, GROUP * g + b + 1)
                act.activation(probs[:, b % 2, 0:KEYS], scores[:, 0:KEYS], ACT.Exp,
                               bias=shift[:, b % 2:b % 2 + 1], scale=D ** -0.5,
                               accum_out=total[:, b % 2:b % 2 + 1]).then_inc(probs_ready, 1)

            def square(g, t):
                act.wait_ge(h_ready, TILES * g + t + 1)
                act.activation(squares, h[:, t % 2], ACT.Square, scale=D ** -0.5,
                               accum_out=meansq[:, t % 2:t % 2 + 1]).then_inc(meansq_ready, 1)

            def tanh(g, t):
                act.wait_ge(z_ready, TILES * g + t + 1)
                act.activation(z[:, t % 2], z[:, t % 2], ACT.Tanh, scale=0.5).then_inc(tanh_ready, 1)

            act.wait_ge(wm_loaded, 16)
            high(wm_hi[:], wm_raw[:]).then_inc(wm_hi_ready, 1)
            split_xT(0, 0)
            split_memT(0, 0)
            split_xT(0, 1)
            split_mem(0, 0)
            act.wait_ge(wmT_loaded, 16)
            high(wmT_hi[:], wmT_raw).then_inc(wmT_hi_ready, 1)
            for c in range(EC):
                act.wait_ge(wga_done, c + 1)
                high(wga_hi[:, c], q_ps[c][:]).then_inc(wga_hi_ready, 1)
            split_xT(0, 2)
            act.wait_ge(padding_ready, 1)

            def group(g, last):
                q_high(g, 0, 0)
                q_high(g, 0, 1)
                q_high(g, 1, 0)
                for b in range(GROUP):
                    ahead = not last or b + 1 < GROUP
                    after = (g, b + 1) if b + 1 < GROUP else (g + 1, 0)
                    if ahead:
                        split_memT(*after)
                    exponentials(g, b)
                    if ahead:
                        split_mem(*after)
                    if b >= 3:
                        square(g, b - 3)
                    if b == 0:
                        q_high(g, 1, 1)
                    if not last and b in (4, 6):
                        unit = (b - 4) // 2
                        act.wait_ge(gate_x_done, TILES * g + (2, 5)[unit])
                        split_xT(g + 1, unit)
                    act.wait_ge(pT_done, GROUP * g + b + 1)
                    high(pT_hi[:, b % 2], probsT).then_inc(pT_hi_ready, 1)
                    if b >= 2:
                        tanh(g, b - 2)
                    act.wait_ge(share_ready, GROUP * g + b + 1)
                    act.wait_ge(am_done, GROUP * g + b + 1)
                    act.activation(am[:], am_ps, ACT.Copy,
                                   scale=share[:, b % 2:b % 2 + 1]).then_inc(am_ready, 1)
                    act.wait_ge(amT_done, GROUP * g + b + 1)
                    high(amT_hi[:, :, b * ROWS:(b + 1) * ROWS], amT_ps).then_inc(amT_hi_ready, 1)
                    if b < 2:
                        q_high(g, 2, b)
                square(g, TILES - 2)
                if not last:
                    act.wait_ge(gate_x_done, TILES * g + TILES)
                    split_xT(g + 1, 2)
                tanh(g, TILES - 1)
                square(g, TILES - 1)

            with act.Fori(0, GROUPS - 1) as g:
                group(g, False)
            group(GROUPS - 1, True)

        @block.vector
        def _(dve):
            def low(out, in_, high):
                return dve.tensor_tensor(out, in_, high.bitcast(F32), ALU.subtract)

            def q_low(g, unit, half):
                c, w = UNITS[unit]
                n = EC * unit + half
                dve.wait_ge(q_hi_ready, PIECES * g + n + 1)
                low(qT_lo[:, half, c:c + w], q_ps[n % 2][:, 0:w],
                    qT_hi[:, half, c:c + w]).then_inc(q_lo_ready, 1)

            def maximum(g, b):
                s = slice(b % 2, b % 2 + 1)
                dve.wait_ge(scores_done, GROUP * g + b + 1)
                dve.tensor_reduce(top[:, s], scores[:, 0:KEYS], AX.X, ALU.max).then_inc(top_ready, 1)
                dve.wait_ge(top_ready, GROUP * g + b + 1)
                dve.tensor_scalar(shift[:, s], top[:, s], -D ** -0.5, None, ALU.mult).then_inc(shift_ready, 1)

            def shares(g, b):
                s = slice(b % 2, b % 2 + 1)
                dve.wait_ge(probs_ready, GROUP * g + b + 1)
                dve.reciprocal(share[:, s], total[:, s]).then_inc(share_ready, 1)

            def pT_low(g, b):
                dve.wait_ge(pT_hi_ready, GROUP * g + b + 1)
                low(pT_lo[:, b % 2], probsT, pT_hi[:, b % 2]).then_inc(pT_lo_ready, 1)

            def amT_low(g, b):
                cols = slice(b * ROWS, (b + 1) * ROWS)
                dve.wait_ge(amT_hi_ready, GROUP * g + b + 1)
                low(amT_lo[:, :, cols], amT_ps, amT_hi[:, :, cols]).then_inc(amT_lo_ready, 1)

            def add_bias(g, t):
                dve.wait_ge(gate_done, TILES * g + t + 1)
                dve.tensor_tensor(z[:, t % 2], gate_ps[t % 2][:], b_gate[:], ALU.add).then_inc(z_ready, 1)

            def gate_context(g, t):
                dve.wait_ge(tanh_ready, TILES * g + t + 1)
                dve.wait_ge(ctx_done, TILES * g + t + 1)
                dve.scalar_tensor_tensor(out=u, in0=z[:, t % 2], scalar=1.0, in1=ctx_ps[:],
                                         op0=ALU.add, op1=ALU.mult).then_inc(u_ready, 1)

            def fuse(g, t):
                dve.wait_ge(x_loaded[t % X_SLOTS], 16 * x_slot_use(g, t))
                dve.wait_ge(u_ready, TILES * g + t + 1)
                dve.scalar_tensor_tensor(out=h[:, t % 2], in0=u, scalar=0.5, in1=x_rows[:, t % X_SLOTS],
                                         op0=ALU.mult, op1=ALU.add).then_inc(h_ready, 1)

            def norm(g, t):
                dve.wait_ge(rstd_ready, TILES * g + t + 1)
                dve.wait_ge(y_stored[t % 2], 16 * (y_slot_use(g, t) + 1))
                dve.scalar_tensor_tensor(out=y[:, t % 2], in0=h[:, t % 2], scalar=rstd[:, t % 2:t % 2 + 1],
                                         in1=norm_w[:], op0=ALU.mult, op1=ALU.mult).then_inc(y_ready, 1)

            dve.memset(probs[:, :, KEYS:KPAD], 0.0).then_inc(padding_ready, 1)
            dve.memset(minus_half[:], -0.5).then_inc(constants_ready, 1)
            dve.memset(eps[:], EPS).then_inc(constants_ready, 1)
            dve.wait_ge(wm_hi_ready, 1)
            low(wm_lo[:], wm_raw[:], wm_hi[:]).then_inc(wm_lo_ready, 1)
            dve.wait_ge(wgx_loaded, 16)
            dve.tensor_copy(wgx_hi[:], wgx_raw[:]).then_inc(wgx_hi_ready, 1)
            dve.wait_ge(wgx_hi_ready, 1)
            low(wgx_lo[:], wgx_raw[:], wgx_hi[:]).then_inc(wgx_lo_ready, 1)
            dve.wait_ge(wmT_hi_ready, 1)
            low(wmT_lo[:], wmT_raw, wmT_hi[:]).then_inc(wmT_lo_ready, 1)
            for c in range(EC):
                dve.wait_ge(wga_hi_ready, c + 1)
                low(wga_lo[:, c], q_ps[c][:], wga_hi[:, c]).then_inc(wga_lo_ready, 1)
            dve.wait_ge(vectors_loaded, 32)

            def group(g):
                q_low(g, 0, 0)
                q_low(g, 0, 1)
                q_low(g, 1, 0)
                for b in range(GROUP):
                    if b >= 3:
                        gate_context(g, b - 3)
                    if b >= 1:
                        amT_low(g, b - 1)
                    if b in (1, 2):
                        q_low(g, 2, b - 1)
                    maximum(g, b)
                    if b >= 3:
                        fuse(g, b - 3)
                    if b == 0:
                        q_low(g, 1, 1)
                    shares(g, b)
                    pT_low(g, b)
                    if b >= 2:
                        add_bias(g, b - 2)
                    if b >= 3:
                        norm(g, b - 3)
                gate_context(g, TILES - 2)
                amT_low(g, GROUP - 1)
                fuse(g, TILES - 2)
                add_bias(g, TILES - 1)
                norm(g, TILES - 2)
                gate_context(g, TILES - 1)
                fuse(g, TILES - 1)
                norm(g, TILES - 1)

            with dve.Fori(0, GROUPS - 1) as g:
                group(g)
            group(GROUPS - 1)

        @block.gpsimd
        def _(pool):
            def low(out, in_, high):
                return pool.tensor_tensor(out, in_, high.bitcast(F32), ALU.subtract)

            def split_xT(g, unit):
                c, n = UNITS[unit]
                pool.wait_ge(xT_hi_ready, len(UNITS) * g + unit + 1)
                low(xT_lo[:, :, c:c + n], xT_raw[:, :, c:c + n], xT_hi[:, :, c:c + n]).then_inc(xT_lo_ready, 1)

            def split_memT(g, b):
                pool.wait_ge(memT_hi_ready, GROUP * g + b + 1)
                low(memT_lo[:, b % 2], memT_raw[:, b % 2], memT_hi[:, b % 2]).then_inc(memT_lo_ready, 1)

            def split_mem(g, b):
                pool.wait_ge(mem_hi_ready, GROUP * g + b + 1)
                low(mem_lo[:, b % 2], mem_raw[:, b % 2], mem_hi[:, b % 2]).then_inc(mem_lo_ready, 1)

            def inverse_rms(g, t):
                s = slice(t % 2, t % 2 + 1)
                pool.wait_ge(meansq_ready, TILES * g + t + 1)
                pool.tensor_tensor(guarded[:, s], meansq[:, s], eps[:], ALU.add).then_inc(guarded_ready, 1)
                pool.wait_ge(guarded_ready, TILES * g + t + 1)
                pool.tensor_tensor(rstd[:, s], guarded[:, s], minus_half[:], ALU.pow).then_inc(rstd_ready, 1)

            pool.memset(ident[:], 0.0).then_inc(blank_ready, 1)
            pool.wait_ge(blank_ready, 1)
            pool.affine_select(out=ident[:], in_=ident[:], compare_op=ALU.not_equal, fill=1.0, base=0,
                               pattern=[[-1, P]], channel_multiplier=1).then_inc(ident_ready, 1)
            pool.wait_ge(constants_ready, 2)
            split_xT(0, 0)
            split_memT(0, 0)
            split_xT(0, 1)
            split_mem(0, 0)
            split_xT(0, 2)

            def group(g, last):
                for b in range(GROUP):
                    ahead = not last or b + 1 < GROUP
                    after = (g, b + 1) if b + 1 < GROUP else (g + 1, 0)
                    if ahead:
                        split_memT(*after)
                    if b >= 3:
                        inverse_rms(g, b - 3)
                    if ahead:
                        split_mem(*after)
                    if not last and b in (4, 6):
                        split_xT(g + 1, (b - 4) // 2)
                inverse_rms(g, TILES - 2)
                if not last:
                    split_xT(g + 1, 2)
                inverse_rms(g, TILES - 1)

            with pool.Fori(0, GROUPS - 1) as g:
                group(g, False)
            group(GROUPS - 1, True)


def kernel(x, ctx_1024, L0_xattn_W_mem, L0_xattn_W_gate, L0_xattn_b_gate, L0_xattn_norm_w):
    import numpy as np
    import concourse.bacc as bacc
    from concourse.bass_utils import run_bass_kernel_spmd

    x, memory, w_mem, w_gate, b_gate, norm_w = (
        np.asarray(a) for a in (x, ctx_1024, L0_xattn_W_mem, L0_xattn_W_gate, L0_xattn_b_gate, L0_xattn_norm_w))

    def chunked(a):
        *lead, rows, n = a.shape
        return np.ascontiguousarray(np.swapaxes(a.reshape(*lead, rows // P, P, n), -3, -2))

    def padded(a, axis, size):
        width = [(0, 0)] * a.ndim
        width[axis] = (0, size - a.shape[axis])
        return np.pad(a, width)

    arrays = {
        "x": np.ascontiguousarray(x.reshape(GROUPS * TILES, P, D)),
        "xT": chunked(np.swapaxes(x.reshape(GROUPS, COLS, D), 1, 2)),
        "mem": chunked(padded(memory, 1, KPAD)),
        "memT": chunked(padded(np.swapaxes(memory, 1, 2), 2, KEVEN)),
        "wm": chunked(w_mem),
        "wmT": chunked(w_mem.T),
        "wgT": chunked(w_gate.T),
        "b": np.ascontiguousarray(b_gate),
        "nw": np.ascontiguousarray(norm_w),
    }
    nc = bacc.Bacc("TRN2", target_bir_lowering=False, num_devices=1)
    args = [nc.dram_tensor(f"in_{n}", a.shape, F32, kind="ExternalInput").ap() for n, a in arrays.items()]
    out = nc.dram_tensor("out", (GROUPS * TILES, P, D), F32, kind="ExternalOutput").ap()
    build_gated_cross_attention(nc, *args, out)
    r = run_bass_kernel_spmd(nc, [{f"in_{n}": a for n, a in arrays.items()}], core_ids=[0])
    return r.results[0]["out"].reshape(BATCHES, ROWS, D)
```

```python
from contextlib import ExitStack

import concourse.bass as bass
from concourse import mybir

F32 = mybir.dt.float32
F32R = mybir.dt.float32r
ACT = mybir.ActivationFunctionType
ALU = mybir.AluOpType
AX = mybir.AxisListType

P = 128
BATCHES, ROWS, D = 32, 112, 512
KEYS, E = 375, 256
EPS = 1e-6

GROUP = 8
GROUPS = BATCHES // GROUP
COLS = GROUP * ROWS
TILES = COLS // P
DC, EC = D // P, E // P
KC = -(-KEYS // P)
KPAD = KC * P
KEVEN = KEYS + KEYS % 2
UNITS = [(0, 256), (256, 320), (576, 320)]
PIECES = len(UNITS) * EC
SPLIT_AT = (4, 6, 7)
X_SLOTS = 4


def unit_of(batch):
    end = (batch + 1) * ROWS
    return next(u for u, (c, n) in enumerate(UNITS) if end <= c + n)


def last_tile_of(unit):
    c, n = UNITS[unit]
    return (c + n - 1) // P


def x_slot_use(g, t):
    slot = t % X_SLOTS
    a_group = len(range(slot, TILES, X_SLOTS))
    return a_group * g + t // X_SLOTS + 1


def y_slot_use(g, t):
    a_group = len(range(t % 2, TILES, 2))
    return a_group * g + t // 2


def build_gated_cross_attention(nc, x_d, xT_d, mem_d, memT_d, wm_d, wmT_d, wgT_d, b_d, nw_d, out_d):
    ctx = ExitStack()
    with ctx:
        def sb(name, shape, dt=F32):
            return ctx.enter_context(nc.sbuf_tensor(name, shape, dt))

        def pb(name, shape):
            return ctx.enter_context(nc.psum_tensor(name, shape, F32))

        def sem(name):
            return ctx.enter_context(nc.semaphore(name))

        ident = sb("ident", [P, P])
        wm_raw = sb("wm_raw", [P, DC, E])
        wm_hi, wm_lo = (sb(f"wm_{s}", [P, DC, E], F32R) for s in ("hi", "lo"))
        wmT_hi, wmT_lo = (sb(f"wmT_{s}", [P, EC, D], F32R) for s in ("hi", "lo"))
        wgx_hi, wgx_lo = (sb(f"wgx_{s}", [P, DC, D], F32R) for s in ("hi", "lo"))
        wga_hi, wga_lo = (sb(f"wga_{s}", [P, EC, D], F32R) for s in ("hi", "lo"))
        b_gate = sb("b_gate", [P, D])
        norm_w = sb("norm_w", [P, D])
        xT_raw = sb("xT_raw", [P, DC, COLS])
        xT_hi, xT_lo = (sb(f"xT_{s}", [P, DC, COLS], F32R) for s in ("hi", "lo"))
        qT_hi, qT_lo = (sb(f"qT_{s}", [P, EC, COLS], F32R) for s in ("hi", "lo"))
        amT_hi, amT_lo = (sb(f"amT_{s}", [P, EC, COLS], F32R) for s in ("hi", "lo"))
        memT_raw = sb("memT_raw", [P, 2, EC, KEVEN])
        memT_hi, memT_lo = (sb(f"memT_{s}", [P, 2, EC, KEVEN], F32R) for s in ("hi", "lo"))
        mem_raw = sb("mem_raw", [P, 2, KC, E])
        mem_hi, mem_lo = (sb(f"mem_{s}", [P, 2, KC, E], F32R) for s in ("hi", "lo"))
        probs = sb("probs", [ROWS, 2, KPAD])
        pT_hi, pT_lo = (sb(f"pT_{s}", [P, 2, KC, ROWS], F32R) for s in ("hi", "lo"))
        am = sb("am", [ROWS, E])
        x_rows = sb("x_rows", [P, X_SLOTS, D])
        work = sb("work", [P, 8, D])
        z, h, y = work[:, 0:2], work[:, 2:4], work[:, 4:6]
        u, squares = work[:, 6], work[:, 7]
        top = sb("top", [ROWS, 2])
        shift = sb("shift", [ROWS, 2])
        total = sb("total", [ROWS, 2])
        share = sb("share", [ROWS, 2])
        meansq = sb("meansq", [P, 2])
        guarded = sb("guarded", [P, 2])
        rstd = sb("rstd", [P, 2])
        minus_half = sb("minus_half", [P, 1])
        eps = sb("eps", [P, 1])
        wga_raw = work[:, 0:DC]
        wmT_raw = work[:, DC:DC + EC]
        wgx_raw = x_rows

        q_ps = [pb(f"q_ps{i}", [P, D]) for i in range(2)]
        score_ps = pb("score_ps", [P, D])
        pT_ps = pb("pT_ps", [P, D])
        am_bank = pb("am_bank", [P, D])
        ctx_ps = pb("ctx_ps", [P, D])
        gate_ps = [pb(f"gate_ps{i}", [P, D]) for i in range(2)]
        wga_ps = [ctx_ps, gate_ps[1]]
        scores = score_ps[0:ROWS, 0:KEVEN]
        probsT = pT_ps[:, 0:KC * ROWS].rearrange("p (c n) -> p c n", c=KC)
        am_ps = am_bank[0:ROWS, 0:E]
        amT_ps = am_bank[:, E:E + EC * ROWS].rearrange("p (c n) -> p c n", c=EC)

        wm_loaded, wga_loaded, wgx_loaded, wmT_loaded, vectors_loaded = map(
            sem, ("wm_loaded", "wga_loaded", "wgx_loaded", "wmT_loaded", "vectors_loaded"))
        wm_hi_ready, wm_lo_ready = sem("wm_hi_ready"), sem("wm_lo_ready")
        wgx_hi_ready, wgx_lo_ready = sem("wgx_hi_ready"), sem("wgx_lo_ready")
        wmT_hi_ready, wmT_lo_ready = sem("wmT_hi_ready"), sem("wmT_lo_ready")
        wga_done, wga_hi_ready, wga_lo_ready = sem("wga_done"), sem("wga_hi_ready"), sem("wga_lo_ready")
        blank_ready, ident_ready, padding_ready = sem("blank_ready"), sem("ident_ready"), sem("padding_ready")
        constants_ready = sem("constants_ready")
        xT_loaded = [sem(f"xT_loaded{i}") for i in range(len(UNITS))]
        memT_loaded = [sem(f"memT_loaded{i}") for i in range(2)]
        mem_loaded = [sem(f"mem_loaded{i}") for i in range(2)]
        x_loaded = [sem(f"x_loaded{i}") for i in range(X_SLOTS)]
        y_stored = [sem(f"y_stored{i}") for i in range(2)]
        xT_hi_ready, xT_lo_ready = sem("xT_hi_ready"), sem("xT_lo_ready")
        memT_hi_ready, memT_lo_ready = sem("memT_hi_ready"), sem("memT_lo_ready")
        mem_hi_ready, mem_lo_ready = sem("mem_hi_ready"), sem("mem_lo_ready")
        q_done, q_hi_ready, q_lo_ready = sem("q_done"), sem("q_hi_ready"), sem("q_lo_ready")
        scores_done, top_ready, shift_ready = sem("scores_done"), sem("top_ready"), sem("shift_ready")
        probs_ready, share_ready = sem("probs_ready"), sem("share_ready")
        pT_done, pT_hi_ready, pT_lo_ready = sem("pT_done"), sem("pT_hi_ready"), sem("pT_lo_ready")
        am_done, am_ready = sem("am_done"), sem("am_ready")
        amT_done, amT_hi_ready, amT_lo_ready = sem("amT_done"), sem("amT_hi_ready"), sem("amT_lo_ready")
        gate_x_done, gate_done, ctx_done = sem("gate_x_done"), sem("gate_done"), sem("ctx_done")
        z_ready, tanh_ready, u_ready, h_ready = sem("z_ready"), sem("tanh_ready"), sem("u_ready"), sem("h_ready")
        meansq_ready, guarded_ready, rstd_ready = sem("meansq_ready"), sem("guarded_ready"), sem("rstd_ready")
        y_ready = sem("y_ready")

        block = ctx.enter_context(nc.Block())

        @block.sync
        def _(sp):
            def load_xT(g, unit):
                c, n = UNITS[unit]
                sp.dma_start(xT_raw[:, :, c:c + n], xT_d[g, :, :, c:c + n]).then_inc(xT_loaded[unit], 16)

            def load_memory(batch, slot):
                sp.dma_start(memT_raw[:, slot], memT_d[batch]).then_inc(memT_loaded[slot], 16)
                sp.dma_start(mem_raw[:, slot], mem_d[batch]).then_inc(mem_loaded[slot], 16)

            def load_x(tile, slot):
                sp.dma_start(x_rows[:, slot], x_d[tile]).then_inc(x_loaded[slot], 16)

            sp.dma_start(wm_raw[:], wm_d).then_inc(wm_loaded, 16)
            load_xT(0, 0)
            load_xT(0, 1)
            sp.dma_start(memT_raw[:, 0], memT_d[0]).then_inc(memT_loaded[0], 16)
            sp.dma_start(wga_raw, wgT_d[:, DC:2 * DC]).then_inc(wga_loaded, 16)
            sp.dma_start(mem_raw[:, 0], mem_d[0]).then_inc(mem_loaded[0], 16)
            sp.dma_start(wgx_raw[:], wgT_d[:, 0:DC]).then_inc(wgx_loaded, 16)
            load_xT(0, 2)
            sp.dma_start(wmT_raw, wmT_d).then_inc(wmT_loaded, 16)
            load_memory(1, 1)
            sp.dma_start(b_gate[:], b_d.partition_broadcast(P)).then_inc(vectors_loaded, 16)
            sp.dma_start(norm_w[:], nw_d.partition_broadcast(P)).then_inc(vectors_loaded, 16)
            for slot in range(2):
                sp.sem_inc(y_stored[slot], 16)
            sp.wait_ge(wgx_hi_ready, 1)
            sp.wait_ge(wgx_lo_ready, 1)
            for t in range(X_SLOTS):
                load_x(t, t)

            def finish(g, t, last):
                sp.wait_ge(h_ready, TILES * g + t + 1)
                if t + X_SLOTS < TILES:
                    load_x(TILES * g + t + X_SLOTS, t % X_SLOTS)
                elif not last:
                    load_x(TILES * (g + 1) + t % X_SLOTS, t % X_SLOTS)
                sp.wait_ge(y_ready, TILES * g + t + 1)
                sp.dma_start(out_d[TILES * g + t], y[:, t % 2]).then_inc(y_stored[t % 2], 16)

            def group(g, last):
                for b in range(GROUP):
                    if not last or b + 2 < GROUP:
                        sp.wait_ge(memT_lo_ready, GROUP * g + b + 1)
                        sp.wait_ge(mem_lo_ready, GROUP * g + b + 1)
                        load_memory(GROUP * g + b + 2, b % 2)
                    if not last and b in (1, 3, 5):
                        unit = b // 2
                        sp.wait_ge(xT_lo_ready, len(UNITS) * g + unit + 1)
                        load_xT(g + 1, unit)
                    if b >= 3:
                        finish(g, b - 3, last)
                finish(g, TILES - 2, last)
                finish(g, TILES - 1, last)

            with sp.Fori(0, GROUPS - 1) as g:
                group(g, False)
            group(GROUPS - 1, True)
            for slot in range(2):
                sp.wait_ge(y_stored[slot], 16 * (1 + y_slot_use(GROUPS, slot)))

        @block.tensor
        def _(pe):
            def product(out, lefts, rights, first=True, last=True):
                n = 3 * len(lefts)
                i = 0
                for (l_hi, l_lo), (r_hi, r_lo) in zip(lefts, rights):
                    for left, right in ((l_hi, r_hi), (l_hi, r_lo), (l_lo, r_hi)):
                        mm = pe.matmul(out, left, right, start=first and i == 0, stop=last and i == n - 1)
                        i += 1
                return mm

            WHOLE, OPEN, CLOSE = (True, True), (True, False), (False, True)

            def chunks_of(part, n):
                first, last = part
                return range(0 if first else n // 2, n if last else n // 2)

            def q_piece(g, unit, half, part=WHOLE):
                n = EC * unit + half
                if half == 0 and part[0]:
                    pe.wait_ge(xT_hi_ready, len(UNITS) * g + unit + 1)
                    pe.wait_ge(xT_lo_ready, len(UNITS) * g + unit + 1)
                if n >= 2 and part[0]:
                    pe.wait_ge(q_lo_ready, PIECES * g + n - 1)
                c, w = UNITS[unit]
                es = slice(half * P, (half + 1) * P)
                mm = product(q_ps[n % 2][:, 0:w],
                             [(wm_hi[:, i, es], wm_lo[:, i, es]) for i in chunks_of(part, DC)],
                             [(xT_hi[:, i, c:c + w], xT_lo[:, i, c:c + w]) for i in chunks_of(part, DC)], *part)
                if part[1]:
                    mm.then_inc(q_done, 1)

            def score(g, b):
                pe.wait_ge(q_lo_ready, PIECES * g + EC * (unit_of(b) + 1))
                pe.wait_ge(memT_hi_ready, GROUP * g + b + 1)
                pe.wait_ge(memT_lo_ready, GROUP * g + b + 1)
                cols = slice(b * ROWS, (b + 1) * ROWS)
                product(scores,
                        [(qT_hi[:, c, cols], qT_lo[:, c, cols]) for c in range(EC)],
                        [(memT_hi[:, b % 2, c], memT_lo[:, b % 2, c]) for c in range(EC)]).then_inc(scores_done, 1)

            def probs_turn(g, b):
                pe.wait_ge(probs_ready, GROUP * g + b + 1)
                for c in range(KC):
                    mm = pe.transpose(probsT[:, c], probs[:, b % 2, c * P:(c + 1) * P], ident[0:ROWS, 0:ROWS])
                mm.then_inc(pT_done, 1)

            def attend(g, b):
                pe.wait_ge(pT_lo_ready, GROUP * g + b + 1)
                pe.wait_ge(mem_hi_ready, GROUP * g + b + 1)
                pe.wait_ge(mem_lo_ready, GROUP * g + b + 1)
                if b > 0:
                    pe.wait_ge(amT_lo_ready, GROUP * g + b)
                product(am_ps,
                        [(pT_hi[:, b % 2, c], pT_lo[:, b % 2, c]) for c in range(KC)],
                        [(mem_hi[:, b % 2, c], mem_lo[:, b % 2, c]) for c in range(KC)]).then_inc(am_done, 1)

            def am_turn(g, b):
                pe.wait_ge(am_ready, GROUP * g + b + 1)
                for c in range(EC):
                    mm = pe.transpose(amT_ps[:, c], am[:, c * P:(c + 1) * P], ident[0:ROWS, 0:ROWS])
                mm.then_inc(amT_done, 1)

            def gate_x(g, t, part=WHOLE):
                pe.wait_ge(wgx_hi_ready, 1)
                pe.wait_ge(wgx_lo_ready, 1)
                pe.wait_ge(wga_lo_ready, EC)
                if t >= 2 and part[0]:
                    pe.wait_ge(z_ready, TILES * g + t - 1)
                cols = slice(t * P, (t + 1) * P)
                mm = product(gate_ps[t % 2][:],
                             [(xT_hi[:, i, cols], xT_lo[:, i, cols]) for i in chunks_of(part, DC)],
                             [(wgx_hi[:, i], wgx_lo[:, i]) for i in chunks_of(part, DC)], part[0], False)
                if part[1]:
                    mm.then_inc(gate_x_done, 1)

            def am_columns(t, part=WHOLE):
                cols = slice(t * P, (t + 1) * P)
                return [(amT_hi[:, c, cols], amT_lo[:, c, cols]) for c in chunks_of(part, EC)]

            def gate_am(g, t):
                pe.wait_ge(amT_lo_ready, GROUP * g + t + 2)
                product(gate_ps[t % 2][:], am_columns(t),
                        [(wga_hi[:, c], wga_lo[:, c]) for c in range(EC)], first=False).then_inc(gate_done, 1)

            def context(g, t, part=WHOLE):
                pe.wait_ge(wmT_hi_ready, 1)
                pe.wait_ge(wmT_lo_ready, 1)
                if t > 0 and part[0]:
                    pe.wait_ge(u_ready, TILES * g + t)
                mm = product(ctx_ps[:], am_columns(t, part),
                             [(wmT_hi[:, c], wmT_lo[:, c]) for c in chunks_of(part, EC)], *part)
                if part[1]:
                    mm.then_inc(ctx_done, 1)

            def fillers(g, b):
                if b == 0:
                    return ([(q_piece, 1, 1)], [(gate_x, 0, OPEN)], [(q_piece, 2, 0, OPEN)])
                if b == 1:
                    return ([(q_piece, 2, 0, CLOSE), (gate_x, 0, CLOSE)], [(gate_x, 1, OPEN)], [(q_piece, 2, 1, OPEN)])
                gates = [(q_piece, 2, 1, CLOSE), (gate_x, 1, CLOSE)] if b == 2 else [(gate_x, b - 1)]
                return (gates, [(gate_am, b - 2)], [(context, b - 2, OPEN if b == GROUP - 1 else WHOLE)])

            def group(g, last):
                for b in range(GROUP):
                    after_scores, after_probs, after_am = fillers(g, b)
                    score(g, b)
                    for what, *which in after_scores:
                        what(g, *which)
                    probs_turn(g, b)
                    for what, *which in after_probs:
                        what(g, *which)
                    attend(g, b)
                    for what, *which in after_am:
                        what(g, *which)
                    am_turn(g, b)
                context(g, TILES - 2, CLOSE)
                if not last:
                    q_piece(g + 1, 0, 0)
                gate_am(g, TILES - 1)
                context(g, TILES - 1)
                if not last:
                    q_piece(g + 1, 0, 1)
                    q_piece(g + 1, 1, 0)

            pe.wait_ge(wm_hi_ready, 1)
            pe.wait_ge(wm_lo_ready, 1)
            q_piece(0, 0, 0)
            q_piece(0, 0, 1)
            q_piece(0, 1, 0)
            pe.wait_ge(wga_loaded, 16)
            for c in range(EC):
                for i in range(DC):
                    mm = pe.matmul(wga_ps[c][:], wm_raw[:, i, c * P:(c + 1) * P], wga_raw[:, i],
                                   start=i == 0, stop=i == DC - 1)
                mm.then_inc(wga_done, 1)
            pe.wait_ge(ident_ready, 1)

            with pe.Fori(0, GROUPS - 1) as g:
                group(g, False)
            group(GROUPS - 1, True)

        @block.scalar
        def _(act):
            def high(out, in_):
                return act.activation(out, in_, ACT.Copy)

            def split_xT(g, unit):
                c, n = UNITS[unit]
                act.wait_ge(xT_loaded[unit], 16 * (g + 1))
                high(xT_hi[:, :, c:c + n], xT_raw[:, :, c:c + n]).then_inc(xT_hi_ready, 1)

            def split_memT(g, b):
                act.wait_ge(memT_loaded[b % 2], 16 * (GROUP // 2 * g + b // 2 + 1))
                high(memT_hi[:, b % 2], memT_raw[:, b % 2]).then_inc(memT_hi_ready, 1)

            def split_mem(g, b):
                act.wait_ge(mem_loaded[b % 2], 16 * (GROUP // 2 * g + b // 2 + 1))
                high(mem_hi[:, b % 2], mem_raw[:, b % 2]).then_inc(mem_hi_ready, 1)

            def q_high(g, unit, half):
                c, w = UNITS[unit]
                n = EC * unit + half
                act.wait_ge(q_done, PIECES * g + n + 1)
                high(qT_hi[:, half, c:c + w], q_ps[n % 2][:, 0:w]).then_inc(q_hi_ready, 1)

            def exponentials(g, b):
                act.wait_ge(shift_ready, GROUP * g + b + 1)
                act.activation(probs[:, b % 2, 0:KEYS], scores[:, 0:KEYS], ACT.Exp,
                               bias=shift[:, b % 2:b % 2 + 1], scale=D ** -0.5,
                               accum_out=total[:, b % 2:b % 2 + 1]).then_inc(probs_ready, 1)

            def square(g, t):
                act.wait_ge(h_ready, TILES * g + t + 1)
                act.activation(squares, h[:, t % 2], ACT.Square, scale=D ** -0.5,
                               accum_out=meansq[:, t % 2:t % 2 + 1]).then_inc(meansq_ready, 1)

            def tanh(g, t):
                act.wait_ge(z_ready, TILES * g + t + 1)
                act.activation(z[:, t % 2], z[:, t % 2], ACT.Tanh, scale=0.5).then_inc(tanh_ready, 1)

            act.wait_ge(wm_loaded, 16)
            high(wm_hi[:], wm_raw[:]).then_inc(wm_hi_ready, 1)
            split_xT(0, 0)
            split_xT(0, 1)
            split_memT(0, 0)
            q_high(0, 0, 0)
            split_mem(0, 0)
            q_high(0, 0, 1)
            q_high(0, 1, 0)
            split_xT(0, 2)
            act.wait_ge(wmT_loaded, 16)
            high(wmT_hi[:], wmT_raw).then_inc(wmT_hi_ready, 1)
            for c in range(EC):
                act.wait_ge(wga_done, c + 1)
                high(wga_hi[:, c], wga_ps[c][:]).then_inc(wga_hi_ready, 1)
            act.wait_ge(padding_ready, 1)

            def group(g, last):
                for b in range(GROUP):
                    ahead = not last or b + 1 < GROUP
                    after = (g, b + 1) if b + 1 < GROUP else (g + 1, 0)
                    if ahead:
                        split_memT(*after)
                    exponentials(g, b)
                    if b > 0 and ahead:
                        split_mem(*after)
                    if b >= 3:
                        square(g, b - 3)
                    if b in (1, 2):
                        q_high(g, 2, b - 1)
                    act.wait_ge(pT_done, GROUP * g + b + 1)
                    high(pT_hi[:, b % 2], probsT).then_inc(pT_hi_ready, 1)
                    if b == 0:
                        q_high(g, 1, 1)
                        split_mem(*after)
                    if not last and b in SPLIT_AT:
                        unit = SPLIT_AT.index(b)
                        act.wait_ge(gate_x_done, TILES * g + last_tile_of(unit) + 1)
                        split_xT(g + 1, unit)
                    if b >= 2:
                        tanh(g, b - 2)
                    act.wait_ge(share_ready, GROUP * g + b + 1)
                    act.wait_ge(am_done, GROUP * g + b + 1)
                    act.activation(am[:], am_ps, ACT.Copy,
                                   scale=share[:, b % 2:b % 2 + 1]).then_inc(am_ready, 1)
                    act.wait_ge(amT_done, GROUP * g + b + 1)
                    high(amT_hi[:, :, b * ROWS:(b + 1) * ROWS], amT_ps).then_inc(amT_hi_ready, 1)
                square(g, TILES - 2)
                if not last:
                    q_high(g + 1, 0, 0)
                tanh(g, TILES - 1)
                if not last:
                    q_high(g + 1, 0, 1)
                square(g, TILES - 1)
                if not last:
                    q_high(g + 1, 1, 0)

            with act.Fori(0, GROUPS - 1) as g:
                group(g, False)
            group(GROUPS - 1, True)

        @block.vector
        def _(dve):
            def low(out, in_, high):
                return dve.tensor_tensor(out, in_, high.bitcast(F32), ALU.subtract)

            def q_low(g, unit, half):
                c, w = UNITS[unit]
                n = EC * unit + half
                dve.wait_ge(q_hi_ready, PIECES * g + n + 1)
                low(qT_lo[:, half, c:c + w], q_ps[n % 2][:, 0:w],
                    qT_hi[:, half, c:c + w]).then_inc(q_lo_ready, 1)

            def maximum(g, b):
                s = slice(b % 2, b % 2 + 1)
                dve.wait_ge(scores_done, GROUP * g + b + 1)
                dve.tensor_reduce(top[:, s], scores[:, 0:KEYS], AX.X, ALU.max).then_inc(top_ready, 1)
                dve.wait_ge(top_ready, GROUP * g + b + 1)
                dve.tensor_scalar(shift[:, s], top[:, s], -D ** -0.5, None, ALU.mult).then_inc(shift_ready, 1)

            def shares(g, b):
                s = slice(b % 2, b % 2 + 1)
                dve.wait_ge(probs_ready, GROUP * g + b + 1)
                dve.reciprocal(share[:, s], total[:, s]).then_inc(share_ready, 1)

            def pT_low(g, b):
                dve.wait_ge(pT_hi_ready, GROUP * g + b + 1)
                low(pT_lo[:, b % 2], probsT, pT_hi[:, b % 2]).then_inc(pT_lo_ready, 1)

            def amT_low(g, b):
                cols = slice(b * ROWS, (b + 1) * ROWS)
                dve.wait_ge(amT_hi_ready, GROUP * g + b + 1)
                low(amT_lo[:, :, cols], amT_ps, amT_hi[:, :, cols]).then_inc(amT_lo_ready, 1)

            def add_bias(g, t):
                dve.wait_ge(gate_done, TILES * g + t + 1)
                dve.tensor_tensor(z[:, t % 2], gate_ps[t % 2][:], b_gate[:], ALU.add).then_inc(z_ready, 1)

            def gate_context(g, t):
                dve.wait_ge(tanh_ready, TILES * g + t + 1)
                dve.wait_ge(ctx_done, TILES * g + t + 1)
                dve.scalar_tensor_tensor(out=u, in0=z[:, t % 2], scalar=1.0, in1=ctx_ps[:],
                                         op0=ALU.add, op1=ALU.mult).then_inc(u_ready, 1)

            def fuse(g, t):
                dve.wait_ge(x_loaded[t % X_SLOTS], 16 * x_slot_use(g, t))
                dve.wait_ge(u_ready, TILES * g + t + 1)
                dve.scalar_tensor_tensor(out=h[:, t % 2], in0=u, scalar=0.5, in1=x_rows[:, t % X_SLOTS],
                                         op0=ALU.mult, op1=ALU.add).then_inc(h_ready, 1)

            def norm(g, t):
                dve.wait_ge(rstd_ready, TILES * g + t + 1)
                dve.wait_ge(y_stored[t % 2], 16 * (y_slot_use(g, t) + 1))
                dve.scalar_tensor_tensor(out=y[:, t % 2], in0=h[:, t % 2], scalar=rstd[:, t % 2:t % 2 + 1],
                                         in1=norm_w[:], op0=ALU.mult, op1=ALU.mult).then_inc(y_ready, 1)

            dve.memset(probs[:, :, KEYS:KPAD], 0.0).then_inc(padding_ready, 1)
            dve.memset(minus_half[:], -0.5).then_inc(constants_ready, 1)
            dve.memset(eps[:], EPS).then_inc(constants_ready, 1)
            dve.wait_ge(wm_hi_ready, 1)
            low(wm_lo[:], wm_raw[:], wm_hi[:]).then_inc(wm_lo_ready, 1)
            for unit in range(2):
                c, n = UNITS[unit]
                dve.wait_ge(xT_hi_ready, unit + 1)
                low(xT_lo[:, :, c:c + n], xT_raw[:, :, c:c + n], xT_hi[:, :, c:c + n]).then_inc(xT_lo_ready, 1)
            q_low(0, 0, 0)
            q_low(0, 0, 1)
            q_low(0, 1, 0)
            dve.wait_ge(wgx_loaded, 16)
            dve.tensor_copy(wgx_hi[:], wgx_raw[:]).then_inc(wgx_hi_ready, 1)
            dve.wait_ge(wgx_hi_ready, 1)
            low(wgx_lo[:], wgx_raw[:], wgx_hi[:]).then_inc(wgx_lo_ready, 1)
            dve.wait_ge(wmT_hi_ready, 1)
            low(wmT_lo[:], wmT_raw, wmT_hi[:]).then_inc(wmT_lo_ready, 1)
            for c in range(EC):
                dve.wait_ge(wga_hi_ready, c + 1)
                low(wga_lo[:, c], wga_ps[c][:], wga_hi[:, c]).then_inc(wga_lo_ready, 1)
            dve.wait_ge(vectors_loaded, 32)

            def group(g, last):
                for b in range(GROUP):
                    if b >= 3:
                        gate_context(g, b - 3)
                    if b >= 1:
                        amT_low(g, b - 1)
                    maximum(g, b)
                    if b in (1, 2):
                        q_low(g, 2, b - 1)
                    if b >= 3:
                        fuse(g, b - 3)
                    shares(g, b)
                    pT_low(g, b)
                    if b == 0:
                        q_low(g, 1, 1)
                    if b >= 2:
                        add_bias(g, b - 2)
                    if b >= 3:
                        norm(g, b - 3)
                amT_low(g, GROUP - 1)
                gate_context(g, TILES - 2)
                fuse(g, TILES - 2)
                if not last:
                    q_low(g + 1, 0, 0)
                add_bias(g, TILES - 1)
                norm(g, TILES - 2)
                gate_context(g, TILES - 1)
                fuse(g, TILES - 1)
                if not last:
                    q_low(g + 1, 0, 1)
                    q_low(g + 1, 1, 0)
                norm(g, TILES - 1)

            with dve.Fori(0, GROUPS - 1) as g:
                group(g, False)
            group(GROUPS - 1, True)

        @block.gpsimd
        def _(pool):
            def low(out, in_, high):
                return pool.tensor_tensor(out, in_, high.bitcast(F32), ALU.subtract)

            def split_xT(g, unit):
                c, n = UNITS[unit]
                pool.wait_ge(xT_hi_ready, len(UNITS) * g + unit + 1)
                low(xT_lo[:, :, c:c + n], xT_raw[:, :, c:c + n], xT_hi[:, :, c:c + n]).then_inc(xT_lo_ready, 1)

            def split_memT(g, b):
                pool.wait_ge(memT_hi_ready, GROUP * g + b + 1)
                low(memT_lo[:, b % 2], memT_raw[:, b % 2], memT_hi[:, b % 2]).then_inc(memT_lo_ready, 1)

            def split_mem(g, b):
                pool.wait_ge(mem_hi_ready, GROUP * g + b + 1)
                low(mem_lo[:, b % 2], mem_raw[:, b % 2], mem_hi[:, b % 2]).then_inc(mem_lo_ready, 1)

            def inverse_rms(g, t):
                s = slice(t % 2, t % 2 + 1)
                pool.wait_ge(meansq_ready, TILES * g + t + 1)
                pool.tensor_tensor(guarded[:, s], meansq[:, s], eps[:], ALU.add).then_inc(guarded_ready, 1)
                pool.wait_ge(guarded_ready, TILES * g + t + 1)
                pool.tensor_tensor(rstd[:, s], guarded[:, s], minus_half[:], ALU.pow).then_inc(rstd_ready, 1)

            pool.memset(ident[:], 0.0).then_inc(blank_ready, 1)
            pool.wait_ge(blank_ready, 1)
            pool.affine_select(out=ident[:], in_=ident[:], compare_op=ALU.not_equal, fill=1.0, base=0,
                               pattern=[[-1, P]], channel_multiplier=1).then_inc(ident_ready, 1)
            pool.wait_ge(constants_ready, 2)
            split_memT(0, 0)
            split_mem(0, 0)
            pool.wait_ge(xT_lo_ready, 2)
            split_xT(0, 2)

            def group(g, last):
                for b in range(GROUP):
                    ahead = not last or b + 1 < GROUP
                    after = (g, b + 1) if b + 1 < GROUP else (g + 1, 0)
                    if ahead:
                        split_memT(*after)
                    if b >= 3:
                        inverse_rms(g, b - 3)
                    if ahead:
                        split_mem(*after)
                    if not last and b in SPLIT_AT:
                        split_xT(g + 1, SPLIT_AT.index(b))
                inverse_rms(g, TILES - 2)
                inverse_rms(g, TILES - 1)

            with pool.Fori(0, GROUPS - 1) as g:
                group(g, False)
            group(GROUPS - 1, True)


def kernel(x, ctx_1024, L0_xattn_W_mem, L0_xattn_W_gate, L0_xattn_b_gate, L0_xattn_norm_w):
    import numpy as np
    import concourse.bacc as bacc
    from concourse.bass_utils import run_bass_kernel_spmd

    x, memory, w_mem, w_gate, b_gate, norm_w = (
        np.asarray(a) for a in (x, ctx_1024, L0_xattn_W_mem, L0_xattn_W_gate, L0_xattn_b_gate, L0_xattn_norm_w))

    def chunked(a):
        *lead, rows, n = a.shape
        return np.ascontiguousarray(np.swapaxes(a.reshape(*lead, rows // P, P, n), -3, -2))

    def padded(a, axis, size):
        width = [(0, 0)] * a.ndim
        width[axis] = (0, size - a.shape[axis])
        return np.pad(a, width)

    arrays = {
        "x": np.ascontiguousarray(x.reshape(GROUPS * TILES, P, D)),
        "xT": chunked(np.swapaxes(x.reshape(GROUPS, COLS, D), 1, 2)),
        "mem": chunked(padded(memory, 1, KPAD)),
        "memT": chunked(padded(np.swapaxes(memory, 1, 2), 2, KEVEN)),
        "wm": chunked(w_mem),
        "wmT": chunked(w_mem.T),
        "wgT": chunked(w_gate.T),
        "b": np.ascontiguousarray(b_gate),
        "nw": np.ascontiguousarray(norm_w),
    }
    nc = bacc.Bacc("TRN2", target_bir_lowering=False, num_devices=1)
    args = [nc.dram_tensor(f"in_{n}", a.shape, F32, kind="ExternalInput").ap() for n, a in arrays.items()]
    out = nc.dram_tensor("out", (GROUPS * TILES, P, D), F32, kind="ExternalOutput").ap()
    build_gated_cross_attention(nc, *args, out)
    r = run_bass_kernel_spmd(nc, [{f"in_{n}": a for n, a in arrays.items()}], core_ids=[0])
    return r.results[0]["out"].reshape(BATCHES, ROWS, D)
```

```python
from contextlib import ExitStack

import concourse.bass as bass
from concourse import mybir

F32 = mybir.dt.float32
F32R = mybir.dt.float32r
ACT = mybir.ActivationFunctionType
ALU = mybir.AluOpType
AX = mybir.AxisListType

P = 128
BATCHES, ROWS, D = 32, 112, 512
KEYS, E = 375, 256
EPS = 1e-6

GROUP = 8
GROUPS = BATCHES // GROUP
COLS = GROUP * ROWS
TILES = COLS // P
DC, EC = D // P, E // P
KC = -(-KEYS // P)
KPAD = KC * P
KEVEN = KEYS + KEYS % 2
UNITS = [(0, 256), (256, 320), (576, 320)]
PIECES = len(UNITS) * EC
WARM_UP = (6, 2)
SPLIT_AT = (4, 6, 7)
ALL = slice(0, D)
HALVES = [slice(0, D // 2), slice(D // 2, D)]
X_SLOTS = 4


def unit_of(batch):
    end = (batch + 1) * ROWS
    return next(u for u, (c, n) in enumerate(UNITS) if end <= c + n)


def last_tile_of(unit):
    c, n = UNITS[unit]
    return (c + n - 1) // P


LAST_SLOT = (TILES - 1) % 2


def x_slot_use(g, t):
    slot = t % X_SLOTS
    a_group = len(range(slot, TILES, X_SLOTS))
    return a_group * g + t // X_SLOTS + 1


def y_slot_use(g, t):
    a_group = len(range(t % 2, TILES, 2))
    return a_group * g + t // 2


def build_gated_cross_attention(nc, x_d, xT_d, mem_d, memT_d, wm_d, wgT_d, b_d, nw_d, out_d):
    ctx = ExitStack()
    with ctx:
        def sb(name, shape, dt=F32):
            return ctx.enter_context(nc.sbuf_tensor(name, shape, dt))

        def pb(name, shape):
            return ctx.enter_context(nc.psum_tensor(name, shape, F32))

        def sem(name):
            return ctx.enter_context(nc.semaphore(name))

        ident = sb("ident", [P, P])
        wm_raw = sb("wm_raw", [P, DC, E])
        wm_hi, wm_lo = (sb(f"wm_{s}", [P, DC, E], F32R) for s in ("hi", "lo"))
        wmT_hi, wmT_lo = (sb(f"wmT_{s}", [P, EC, D], F32R) for s in ("hi", "lo"))
        wgx_hi, wgx_lo = (sb(f"wgx_{s}", [P, DC, D], F32R) for s in ("hi", "lo"))
        wga_hi, wga_lo = (sb(f"wga_{s}", [P, EC, D], F32R) for s in ("hi", "lo"))
        wgc_hi, wgc_lo = (sb(f"wgc_{s}", [P, DC, D], F32R) for s in ("hi", "lo"))
        zeros = sb("zeros", [P, D], mybir.dt.bfloat16)
        b_gate = sb("b_gate", [P, D])
        norm_w = sb("norm_w", [P, D])
        xT_raw = sb("xT_raw", [P, DC, COLS])
        xT_hi, xT_lo = (sb(f"xT_{s}", [P, DC, COLS], F32R) for s in ("hi", "lo"))
        qT_hi, qT_lo = (sb(f"qT_{s}", [P, EC, COLS], F32R) for s in ("hi", "lo"))
        amT_hi, amT_lo = (sb(f"amT_{s}", [P, EC, COLS], F32R) for s in ("hi", "lo"))
        memT_raw = sb("memT_raw", [P, 2, EC, KEVEN])
        memT_hi, memT_lo = (sb(f"memT_{s}", [P, 2, EC, KEVEN], F32R) for s in ("hi", "lo"))
        mem_raw = sb("mem_raw", [P, 2, KC, E])
        mem_hi, mem_lo = (sb(f"mem_{s}", [P, 2, KC, E], F32R) for s in ("hi", "lo"))
        probs = sb("probs", [ROWS, 2, KPAD])
        pT_hi, pT_lo = (sb(f"pT_{s}", [P, 2, KC, ROWS], F32R) for s in ("hi", "lo"))
        am = sb("am", [ROWS, E])
        x_rows = sb("x_rows", [P, X_SLOTS, D])
        work = sb("work", [P, 8, D])
        z, h, y = work[:, 0:2], work[:, 2:4], work[:, 4:6]
        u, squares = work[:, 6], work[:, 7]
        top = sb("top", [ROWS, 2])
        shift = sb("shift", [ROWS, 2])
        total = sb("total", [ROWS, 2])
        share = sb("share", [ROWS, 2])
        meansq = sb("meansq", [P, 4])
        guarded = sb("guarded", [P, 4])
        rstd = sb("rstd", [P, 2])
        minus_half = sb("minus_half", [P, 1])
        eps = sb("eps", [P, 1])
        wgc_raw = work[:, 0:DC]
        wgx_raw = x_rows

        q_ps = [pb(f"q_ps{i}", [P, D]) for i in range(2)]
        score_ps = pb("score_ps", [P, D])
        pT_ps = pb("pT_ps", [P, D])
        am_bank = pb("am_bank", [P, D])
        ctx_ps = pb("ctx_ps", [P, D])
        gate_ps = [pb(f"gate_ps{i}", [P, D]) for i in range(2)]
        wga_ps = [ctx_ps, gate_ps[1]]
        wmT_ps = [pT_ps, am_bank]
        late_ps = [ctx_ps, gate_ps[LAST_SLOT - 1]]
        scores = score_ps[0:ROWS, 0:KEVEN]
        probsT = pT_ps[:, 0:KC * ROWS].rearrange("p (c n) -> p c n", c=KC)
        am_ps = am_bank[0:ROWS, 0:E]
        amT_ps = am_bank[:, E:E + EC * ROWS].rearrange("p (c n) -> p c n", c=EC)

        wmT_done, vectors_loaded = sem("wmT_done"), sem("vectors_loaded")
        wm_loaded = [sem(f"wm_loaded{i}") for i in range(2)]
        wgx_loaded = [sem(f"wgx_loaded{i}") for i in range(2)]
        wgc_loaded = [sem(f"wgc_loaded{i}") for i in range(2)]
        x0_loaded, x0_hi_ready, x0_lo_ready = sem("x0_loaded"), sem("x0_hi_ready"), sem("x0_lo_ready")
        wgc_hi_ready, wgc_lo_ready = sem("wgc_hi_ready"), sem("wgc_lo_ready")
        zeros_ready = sem("zeros_ready")
        wm_hi_ready, wm_lo_ready = sem("wm_hi_ready"), sem("wm_lo_ready")
        wgx_hi_ready, wgx_lo_ready = sem("wgx_hi_ready"), sem("wgx_lo_ready")
        wmT_hi_ready, wmT_lo_ready = sem("wmT_hi_ready"), sem("wmT_lo_ready")
        wga_done, wga_hi_ready, wga_lo_ready = sem("wga_done"), sem("wga_hi_ready"), sem("wga_lo_ready")
        blank_ready, ident_ready, padding_ready = sem("blank_ready"), sem("ident_ready"), sem("padding_ready")
        constants_ready = sem("constants_ready")
        xT_loaded = [sem(f"xT_loaded{i}") for i in range(len(UNITS))]
        memT_loaded = [sem(f"memT_loaded{i}") for i in range(2)]
        mem_loaded = [sem(f"mem_loaded{i}") for i in range(2)]
        x_loaded = [sem(f"x_loaded{i}") for i in range(X_SLOTS)]
        y_stored = [sem(f"y_stored{i}") for i in range(2)]
        xT_hi_ready, xT_lo_ready = sem("xT_hi_ready"), sem("xT_lo_ready")
        memT_hi_ready, memT_lo_ready = sem("memT_hi_ready"), sem("memT_lo_ready")
        mem_hi_ready, mem_lo_ready = sem("mem_hi_ready"), sem("mem_lo_ready")
        q_done, q_hi_ready, q_lo_ready = sem("q_done"), sem("q_hi_ready"), sem("q_lo_ready")
        scores_done, top_ready, shift_ready = sem("scores_done"), sem("top_ready"), sem("shift_ready")
        probs_ready, share_ready = sem("probs_ready"), sem("share_ready")
        pT_done, pT_hi_ready, pT_lo_ready = sem("pT_done"), sem("pT_hi_ready"), sem("pT_lo_ready")
        am_done, am_ready = sem("am_done"), sem("am_ready")
        amT_done, amT_hi_ready, amT_lo_ready = sem("amT_done"), sem("amT_hi_ready"), sem("amT_lo_ready")
        gate_x_done, gate_done, ctx_done = sem("gate_x_done"), sem("gate_done"), sem("ctx_done")
        z_ready, tanh_ready, u_ready, h_ready = sem("z_ready"), sem("tanh_ready"), sem("u_ready"), sem("h_ready")
        meansq_ready, guarded_ready, rstd_ready = sem("meansq_ready"), sem("guarded_ready"), sem("rstd_ready")
        y_ready = sem("y_ready")

        block = ctx.enter_context(nc.Block())

        @block.sync
        def _(sp):
            def load_xT(g, unit):
                c, n = UNITS[unit]
                sp.dma_start(xT_raw[:, :, c:c + n], xT_d[g, :, :, c:c + n]).then_inc(xT_loaded[unit], 16)

            def load_memory(batch, slot):
                sp.dma_start(memT_raw[:, slot], memT_d[batch]).then_inc(memT_loaded[slot], 16)
                sp.dma_start(mem_raw[:, slot], mem_d[batch]).then_inc(mem_loaded[slot], 16)

            def load_memory_after(n, slot):
                sp.wait_ge(memT_lo_ready, n + 1)
                sp.wait_ge(mem_lo_ready, n + 1)
                load_memory(n + 2, slot)

            def load_x(tile, slot):
                sp.dma_start(x_rows[:, slot], x_d[tile]).then_inc(x_loaded[slot], 16)

            half = DC // 2

            def load_wgx(i):
                sp.dma_start(wgx_raw[:, half * i:half * (i + 1)],
                             wgT_d[:, half * i:half * (i + 1)]).then_inc(wgx_loaded[i], 16)

            c, n = UNITS[0]
            sp.dma_start(wm_raw[:, 0:half], wm_d[:, 0:half]).then_inc(wm_loaded[0], 16)
            sp.dma_start(xT_raw[:, 0:half, c:c + n], xT_d[0, :, 0:half, c:c + n]).then_inc(x0_loaded, 16)
            sp.dma_start(wm_raw[:, half:DC], wm_d[:, half:DC]).then_inc(wm_loaded[1], 16)
            sp.dma_start(xT_raw[:, half:DC, c:c + n], xT_d[0, :, half:DC, c:c + n]).then_inc(xT_loaded[0], 16)
            for i in range(2):
                sp.dma_start(wgc_raw[:, half * i:half * (i + 1)],
                             wgT_d[:, DC + half * i:DC + half * (i + 1)]).then_inc(wgc_loaded[i], 16)
            sp.dma_start(memT_raw[:, 0], memT_d[0]).then_inc(memT_loaded[0], 16)
            load_xT(0, 1)
            load_wgx(0)
            sp.dma_start(mem_raw[:, 0], mem_d[0]).then_inc(mem_loaded[0], 16)
            load_xT(0, 2)
            load_wgx(1)
            load_memory(1, 1)
            load_memory_after(0, 0)
            sp.dma_start(b_gate[:], b_d.partition_broadcast(P)).then_inc(vectors_loaded, 16)
            sp.dma_start(norm_w[:], nw_d.partition_broadcast(P)).then_inc(vectors_loaded, 16)
            for slot in range(2):
                sp.sem_inc(y_stored[slot], 16)
            sp.wait_ge(wgx_lo_ready, DC)
            for t in range(X_SLOTS):
                load_x(t, t)

            def finish(g, t, last):
                sp.wait_ge(h_ready, TILES * g + t + 1)
                if t + X_SLOTS < TILES:
                    load_x(TILES * g + t + X_SLOTS, t % X_SLOTS)
                elif not last:
                    load_x(TILES * (g + 1) + t % X_SLOTS, t % X_SLOTS)
                sp.wait_ge(y_ready, TILES * g + t + 1)
                sp.dma_start(out_d[TILES * g + t], y[:, t % 2]).then_inc(y_stored[t % 2], 16)

            def group(g, last):
                for b in range(GROUP):
                    if not last or b + 3 < GROUP:
                        load_memory_after(GROUP * g + b + 1, (b + 1) % 2)
                    if not last and b in (1, 3, 5):
                        unit = b // 2
                        sp.wait_ge(xT_lo_ready, len(UNITS) * g + unit + 1)
                        load_xT(g + 1, unit)
                    if b >= 3:
                        finish(g, b - 3, last)
                finish(g, TILES - 2, last)
                if not last:
                    finish(g, TILES - 1, last)

            with sp.Fori(0, GROUPS - 1) as g:
                group(g, False)
            group(GROUPS - 1, True)
            for i, cols in enumerate(HALVES):
                sp.wait_ge(y_ready, TILES * GROUPS + i)
                sp.dma_start(out_d[TILES * GROUPS - 1][:, cols],
                             y[:, LAST_SLOT, cols]).then_inc(y_stored[LAST_SLOT], 16)
            for slot in range(2):
                sp.wait_ge(y_stored[slot], 16 * (1 + y_slot_use(GROUPS, slot) + (slot == LAST_SLOT)))

        @block.tensor
        def _(pe):
            def product(out, lefts, rights, first=True, last=True):
                n = 3 * len(lefts)
                i = 0
                for (l_hi, l_lo), (r_hi, r_lo) in zip(lefts, rights):
                    for left, right in ((l_hi, r_hi), (l_hi, r_lo), (l_lo, r_hi)):
                        mm = pe.matmul(out, left, right, start=first and i == 0, stop=last and i == n - 1)
                        i += 1
                return mm

            WHOLE, OPEN, CLOSE = (0, 4), (0, 2), (2, 4)

            def chunks_of(part, n):
                return range(part[0] * n // 4, part[1] * n // 4)

            def q_product(unit, half, part):
                c, w = UNITS[unit]
                es = slice(half * P, (half + 1) * P)
                mm = product(q_ps[(EC * unit + half) % 2][:, 0:w],
                             [(wm_hi[:, i, es], wm_lo[:, i, es]) for i in chunks_of(part, DC)],
                             [(xT_hi[:, i, c:c + w], xT_lo[:, i, c:c + w]) for i in chunks_of(part, DC)],
                             part[0] == 0, part[1] == 4)
                if part[1] == 4:
                    mm.then_inc(q_done, 1)

            def q_piece(g, unit, half, part=WHOLE):
                n = EC * unit + half
                if half == 0 and part[0] == 0:
                    pe.wait_ge(xT_hi_ready, len(UNITS) * g + unit + 1)
                    pe.wait_ge(xT_lo_ready, len(UNITS) * g + unit + 1)
                if n >= 2 and part[0] == 0:
                    pe.wait_ge(q_lo_ready, PIECES * g + n - 1)
                q_product(unit, half, part)

            def score(g, b):
                pe.wait_ge(q_lo_ready, PIECES * g + EC * (unit_of(b) + 1))
                pe.wait_ge(memT_hi_ready, GROUP * g + b + 1)
                pe.wait_ge(memT_lo_ready, GROUP * g + b + 1)
                cols = slice(b * ROWS, (b + 1) * ROWS)
                product(scores,
                        [(qT_hi[:, c, cols], qT_lo[:, c, cols]) for c in range(EC)],
                        [(memT_hi[:, b % 2, c], memT_lo[:, b % 2, c]) for c in range(EC)]).then_inc(scores_done, 1)

            def probs_turn(g, b):
                pe.wait_ge(probs_ready, GROUP * g + b + 1)
                for c in range(KC):
                    mm = pe.transpose(probsT[:, c], probs[:, b % 2, c * P:(c + 1) * P], ident[0:ROWS, 0:ROWS])
                mm.then_inc(pT_done, 1)

            def attend(g, b):
                pe.wait_ge(pT_lo_ready, GROUP * g + b + 1)
                pe.wait_ge(mem_hi_ready, GROUP * g + b + 1)
                pe.wait_ge(mem_lo_ready, GROUP * g + b + 1)
                if b > 0:
                    pe.wait_ge(amT_lo_ready, GROUP * g + b)
                product(am_ps,
                        [(pT_hi[:, b % 2, c], pT_lo[:, b % 2, c]) for c in range(KC)],
                        [(mem_hi[:, b % 2, c], mem_lo[:, b % 2, c]) for c in range(KC)]).then_inc(am_done, 1)

            def am_turn(g, b):
                pe.wait_ge(am_ready, GROUP * g + b + 1)
                for c in range(EC):
                    mm = pe.transpose(amT_ps[:, c], am[:, c * P:(c + 1) * P], ident[0:ROWS, 0:ROWS])
                mm.then_inc(amT_done, 1)

            def gate_x(g, t, part=WHOLE):
                pe.wait_ge(wgx_lo_ready, part[1] * DC // 4)
                if t == 1:
                    pe.wait_ge(wga_lo_ready, EC)
                if t >= 2 and part[0] == 0:
                    pe.wait_ge(z_ready, TILES * g + t - 1)
                cols = slice(t * P, (t + 1) * P)
                mm = product(gate_ps[t % 2][:],
                             [(xT_hi[:, i, cols], xT_lo[:, i, cols]) for i in chunks_of(part, DC)],
                             [(wgx_hi[:, i], wgx_lo[:, i]) for i in chunks_of(part, DC)], part[0] == 0, False)
                if part[1] == 4:
                    mm.then_inc(gate_x_done, 1)

            def am_columns(t, part=WHOLE):
                cols = slice(t * P, (t + 1) * P)
                return [(amT_hi[:, c, cols], amT_lo[:, c, cols]) for c in chunks_of(part, EC)]

            def gate_am(g, t):
                pe.wait_ge(amT_lo_ready, GROUP * g + t + 2)
                product(gate_ps[t % 2][:], am_columns(t),
                        [(wga_hi[:, c], wga_lo[:, c]) for c in range(EC)], first=False).then_inc(gate_done, 1)

            def context(g, t, part=WHOLE, cols=ALL, bank=ctx_ps):
                pe.wait_ge(wmT_lo_ready, EC)
                if t > 0 and part[0] == 0:
                    pe.wait_ge(u_ready, TILES * g + t)
                mm = product(bank[:, cols], am_columns(t, part),
                             [(wmT_hi[:, c, cols], wmT_lo[:, c, cols]) for c in chunks_of(part, EC)],
                             part[0] == 0, part[1] == 4)
                if part[1] == 4:
                    mm.then_inc(ctx_done, 1)

            def fillers(g, b, last):
                if b == 0:
                    return ([(q_piece, 1, 1)], [(gate_x, 0, OPEN)], [(q_piece, 2, 0, OPEN)])
                if b == 1:
                    return ([(q_piece, 2, 0, CLOSE), (gate_x, 0, CLOSE)], [(gate_x, 1, OPEN)],
                            [(q_piece, 2, 1, OPEN)])
                if b == GROUP - 1 and last:
                    return ([(gate_x, b - 1, (0, 3))], [(gate_am, b - 2)], [(context, b - 2, OPEN)])
                gates = [(q_piece, 2, 1, CLOSE), (gate_x, 1, CLOSE)] if b == 2 else [(gate_x, b - 1)]
                return (gates, [(gate_am, b - 2)], [(context, b - 2)])

            def group(g, last):
                for b in range(GROUP):
                    after_scores, after_probs, after_am = fillers(g, b, last)
                    if b > 0:
                        score(g, b)
                    for what, *which in after_scores:
                        what(g, *which)
                    probs_turn(g, b)
                    for what, *which in after_probs:
                        what(g, *which)
                    attend(g, b)
                    for what, *which in after_am:
                        what(g, *which)
                    am_turn(g, b)
                if last:
                    context(g, TILES - 2, CLOSE)
                    gate_x(g, TILES - 1, (3, 4))
                    gate_am(g, TILES - 1)
                    for cols, bank in zip(HALVES, late_ps):
                        context(g, TILES - 1, cols=cols, bank=bank)
                else:
                    q_piece(g + 1, 0, 0)
                    gate_am(g, TILES - 1)
                    context(g, TILES - 1)
                    q_piece(g + 1, 0, 1)
                    q_piece(g + 1, 1, 0)
                    score(g + 1, 0)

            def warm_up(products):
                for _ in range(products):
                    pe.matmul(score_ps[:], zeros[:, 0:P], zeros[:], start=True, stop=True)

            def turn_wm(half):
                pe.wait_ge(wm_loaded[half], 16)
                for c in range(EC):
                    for i in range(half * DC // 2, (half + 1) * DC // 2):
                        mm = pe.transpose(wmT_ps[c][:, i * P:(i + 1) * P], wm_raw[:, i, c * P:(c + 1) * P], ident[:])
                mm.then_inc(wmT_done, 1)

            pe.wait_ge(zeros_ready, 1)
            warm_up(WARM_UP[0])
            pe.wait_ge(ident_ready, 1)
            turn_wm(0)
            warm_up(WARM_UP[1])
            pe.wait_ge(wm_lo_ready, 1)
            pe.wait_ge(x0_lo_ready, 1)
            q_product(0, 0, OPEN)
            turn_wm(1)
            pe.wait_ge(wm_lo_ready, 2)
            pe.wait_ge(xT_lo_ready, 1)
            q_product(0, 0, CLOSE)
            q_piece(0, 0, 1)
            for c in range(EC):
                for i in range(DC):
                    pe.wait_ge(wgc_hi_ready, i + 1)
                    pe.wait_ge(wgc_lo_ready, i + 1)
                    es = slice(c * P, (c + 1) * P)
                    mm = product(wga_ps[c][:], [(wm_hi[:, i, es], wm_lo[:, i, es])], [(wgc_hi[:, i], wgc_lo[:, i])],
                                 i == 0, i == DC - 1)
                mm.then_inc(wga_done, 1)
            score(0, 0)
            q_piece(0, 1, 0)
            pe.wait_ge(padding_ready, 1)

            with pe.Fori(0, GROUPS - 1) as g:
                group(g, False)
            group(GROUPS - 1, True)

        @block.scalar
        def _(act):
            def high(out, in_):
                return act.activation(out, in_, ACT.Copy)

            def split_xT(g, unit):
                c, n = UNITS[unit]
                act.wait_ge(xT_loaded[unit], 16 * (g + 1))
                high(xT_hi[:, :, c:c + n], xT_raw[:, :, c:c + n]).then_inc(xT_hi_ready, 1)

            def split_memT(g, b):
                act.wait_ge(memT_loaded[b % 2], 16 * (GROUP // 2 * g + b // 2 + 1))
                high(memT_hi[:, b % 2], memT_raw[:, b % 2]).then_inc(memT_hi_ready, 1)

            def split_mem(g, b):
                act.wait_ge(mem_loaded[b % 2], 16 * (GROUP // 2 * g + b // 2 + 1))
                high(mem_hi[:, b % 2], mem_raw[:, b % 2]).then_inc(mem_hi_ready, 1)

            def q_high(g, unit, half):
                c, w = UNITS[unit]
                n = EC * unit + half
                act.wait_ge(q_done, PIECES * g + n + 1)
                high(qT_hi[:, half, c:c + w], q_ps[n % 2][:, 0:w]).then_inc(q_hi_ready, 1)

            def exponentials(g, b):
                act.wait_ge(shift_ready, GROUP * g + b + 1)
                act.activation(probs[:, b % 2, 0:KEYS], scores[:, 0:KEYS], ACT.Exp,
                               bias=shift[:, b % 2:b % 2 + 1], scale=D ** -0.5,
                               accum_out=total[:, b % 2:b % 2 + 1]).then_inc(probs_ready, 1)

            def square(g, t, cols=ALL, i=0):
                slot = t % 2 if cols == ALL else 2 + i
                act.wait_ge(h_ready, TILES * g + t + 1 + i)
                act.activation(squares[:, cols], h[:, t % 2, cols], ACT.Square, scale=D ** -0.5,
                               accum_out=meansq[:, slot:slot + 1]).then_inc(meansq_ready, 1)

            def tanh(g, t, cols=ALL, i=0):
                act.wait_ge(z_ready, TILES * g + t + 1 + i)
                act.activation(z[:, t % 2, cols], z[:, t % 2, cols], ACT.Tanh, scale=0.5).then_inc(tanh_ready, 1)

            half = DC // 2

            def wga_high(c):
                act.wait_ge(wga_done, c + 1)
                high(wga_hi[:, c], wga_ps[c][:]).then_inc(wga_hi_ready, 1)

            def wgx_high(i):
                act.wait_ge(wgx_loaded[i // half], 16)
                high(wgx_hi[:, i], wgx_raw[:, i]).then_inc(wgx_hi_ready, 1)

            c, n = UNITS[0]
            act.wait_ge(wm_loaded[0], 16)
            high(wm_hi[:, 0:half], wm_raw[:, 0:half]).then_inc(wm_hi_ready, 1)
            act.wait_ge(x0_loaded, 16)
            high(xT_hi[:, 0:half, c:c + n], xT_raw[:, 0:half, c:c + n]).then_inc(x0_hi_ready, 1)
            act.wait_ge(wm_loaded[1], 16)
            high(wm_hi[:, half:DC], wm_raw[:, half:DC]).then_inc(wm_hi_ready, 1)
            act.wait_ge(xT_loaded[0], 16)
            high(xT_hi[:, half:DC, c:c + n], xT_raw[:, half:DC, c:c + n]).then_inc(xT_hi_ready, 1)

            for i in range(DC):
                act.wait_ge(wgc_loaded[i // half], 16)
                high(wgc_hi[:, i], wgc_raw[:, i]).then_inc(wgc_hi_ready, 1)
                if i == half - 1:
                    q_high(0, 0, 0)
            q_high(0, 0, 1)
            act.wait_ge(wmT_done, 2)
            for c in range(EC):
                high(wmT_hi[:, c], wmT_ps[c][:]).then_inc(wmT_hi_ready, 1)
            split_memT(0, 0)
            split_xT(0, 1)
            wga_high(0)
            for i in range(half):
                wgx_high(i)
            split_mem(0, 0)
            wga_high(1)
            split_xT(0, 2)
            exponentials(0, 0)
            q_high(0, 1, 0)
            for i in range(half, DC):
                wgx_high(i)

            def group(g, last):
                for b in range(GROUP):
                    ahead = not last or b + 1 < GROUP
                    after = (g, b + 1) if b + 1 < GROUP else (g + 1, 0)
                    if b > 0:
                        if ahead:
                            split_memT(*after)
                        exponentials(g, b)
                        if ahead:
                            split_mem(*after)
                    if b >= 3:
                        square(g, b - 3)
                    if b in (1, 2):
                        q_high(g, 2, b - 1)
                    act.wait_ge(pT_done, GROUP * g + b + 1)
                    high(pT_hi[:, b % 2], probsT).then_inc(pT_hi_ready, 1)
                    if b == 0:
                        split_memT(*after)
                        q_high(g, 1, 1)
                        split_mem(*after)
                    if not last and b in SPLIT_AT:
                        unit = SPLIT_AT.index(b)
                        act.wait_ge(gate_x_done, TILES * g + last_tile_of(unit) + 1)
                        split_xT(g + 1, unit)
                    act.wait_ge(share_ready, GROUP * g + b + 1)
                    act.wait_ge(am_done, GROUP * g + b + 1)
                    act.activation(am[:], am_ps, ACT.Copy,
                                   scale=share[:, b % 2:b % 2 + 1]).then_inc(am_ready, 1)
                    if b >= 2:
                        tanh(g, b - 2)
                    act.wait_ge(amT_done, GROUP * g + b + 1)
                    high(amT_hi[:, :, b * ROWS:(b + 1) * ROWS], amT_ps).then_inc(amT_hi_ready, 1)
                square(g, TILES - 2)
                if last:
                    for i, cols in enumerate(HALVES):
                        tanh(g, TILES - 1, cols, i)
                    for i, cols in enumerate(HALVES):
                        square(g, TILES - 1, cols, i)
                else:
                    q_high(g + 1, 0, 0)
                    tanh(g, TILES - 1)
                    q_high(g + 1, 0, 1)
                    square(g, TILES - 1)
                    q_high(g + 1, 1, 0)
                    exponentials(g + 1, 0)

            with act.Fori(0, GROUPS - 1) as g:
                group(g, False)
            group(GROUPS - 1, True)

        @block.vector
        def _(dve):
            def low(out, in_, high):
                return dve.tensor_tensor(out, in_, high.bitcast(F32), ALU.subtract)

            def q_low(g, unit, half):
                c, w = UNITS[unit]
                n = EC * unit + half
                dve.wait_ge(q_hi_ready, PIECES * g + n + 1)
                low(qT_lo[:, half, c:c + w], q_ps[n % 2][:, 0:w],
                    qT_hi[:, half, c:c + w]).then_inc(q_lo_ready, 1)

            def maximum(g, b):
                s = slice(b % 2, b % 2 + 1)
                dve.wait_ge(scores_done, GROUP * g + b + 1)
                dve.tensor_reduce(top[:, s], scores[:, 0:KEYS], AX.X, ALU.max).then_inc(top_ready, 1)
                dve.wait_ge(top_ready, GROUP * g + b + 1)
                dve.tensor_scalar(shift[:, s], top[:, s], -D ** -0.5, None, ALU.mult).then_inc(shift_ready, 1)

            def shares(g, b):
                s = slice(b % 2, b % 2 + 1)
                dve.wait_ge(probs_ready, GROUP * g + b + 1)
                dve.reciprocal(share[:, s], total[:, s]).then_inc(share_ready, 1)

            def pT_low(g, b):
                dve.wait_ge(pT_hi_ready, GROUP * g + b + 1)
                low(pT_lo[:, b % 2], probsT, pT_hi[:, b % 2]).then_inc(pT_lo_ready, 1)

            def amT_low(g, b):
                cols = slice(b * ROWS, (b + 1) * ROWS)
                dve.wait_ge(amT_hi_ready, GROUP * g + b + 1)
                low(amT_lo[:, :, cols], amT_ps, amT_hi[:, :, cols]).then_inc(amT_lo_ready, 1)

            def add_bias(g, t, cols=ALL):
                dve.wait_ge(vectors_loaded, 32)
                dve.wait_ge(gate_done, TILES * g + t + 1)
                dve.tensor_tensor(z[:, t % 2, cols], gate_ps[t % 2][:, cols], b_gate[:, cols],
                                  ALU.add).then_inc(z_ready, 1)

            def gate_context(g, t, cols=ALL, i=0, bank=ctx_ps):
                dve.wait_ge(tanh_ready, TILES * g + t + 1 + i)
                dve.wait_ge(ctx_done, TILES * g + t + 1 + i)
                dve.scalar_tensor_tensor(out=u[:, cols], in0=z[:, t % 2, cols], scalar=1.0, in1=bank[:, cols],
                                         op0=ALU.add, op1=ALU.mult).then_inc(u_ready, 1)

            def fuse(g, t, cols=ALL, i=0):
                dve.wait_ge(x_loaded[t % X_SLOTS], 16 * x_slot_use(g, t))
                dve.wait_ge(u_ready, TILES * g + t + 1 + i)
                dve.scalar_tensor_tensor(out=h[:, t % 2, cols], in0=u[:, cols], scalar=0.5,
                                         in1=x_rows[:, t % X_SLOTS, cols],
                                         op0=ALU.mult, op1=ALU.add).then_inc(h_ready, 1)

            def norm(g, t, cols=ALL):
                dve.wait_ge(rstd_ready, TILES * g + t + 1)
                dve.wait_ge(y_stored[t % 2], 16 * (y_slot_use(g, t) + 1))
                dve.scalar_tensor_tensor(out=y[:, t % 2, cols], in0=h[:, t % 2, cols],
                                         scalar=rstd[:, t % 2:t % 2 + 1], in1=norm_w[:, cols],
                                         op0=ALU.mult, op1=ALU.mult).then_inc(y_ready, 1)

            def wmT_low(c):
                dve.wait_ge(wmT_hi_ready, c + 1)
                low(wmT_lo[:, c], wmT_ps[c][:], wmT_hi[:, c]).then_inc(wmT_lo_ready, 1)

            def wga_low(c):
                dve.wait_ge(wga_hi_ready, c + 1)
                low(wga_lo[:, c], wga_ps[c][:], wga_hi[:, c]).then_inc(wga_lo_ready, 1)

            def wgx_low(i):
                dve.wait_ge(wgx_hi_ready, i + 1)
                low(wgx_lo[:, i], wgx_raw[:, i], wgx_hi[:, i]).then_inc(wgx_lo_ready, 1)

            dve.memset(zeros[:], 0.0).then_inc(zeros_ready, 1)
            dve.memset(probs[:, :, KEYS:KPAD], 0.0).then_inc(padding_ready, 1)
            dve.memset(minus_half[:], -0.5).then_inc(constants_ready, 1)
            dve.memset(eps[:], EPS).then_inc(constants_ready, 1)
            half = DC // 2
            c, n = UNITS[0]
            dve.wait_ge(wm_hi_ready, 1)
            low(wm_lo[:, 0:half], wm_raw[:, 0:half], wm_hi[:, 0:half]).then_inc(wm_lo_ready, 1)
            dve.wait_ge(x0_hi_ready, 1)
            low(xT_lo[:, 0:half, c:c + n], xT_raw[:, 0:half, c:c + n],
                xT_hi[:, 0:half, c:c + n]).then_inc(x0_lo_ready, 1)
            dve.wait_ge(wm_hi_ready, 2)
            low(wm_lo[:, half:DC], wm_raw[:, half:DC], wm_hi[:, half:DC]).then_inc(wm_lo_ready, 1)
            dve.wait_ge(xT_hi_ready, 1)
            low(xT_lo[:, half:DC, c:c + n], xT_raw[:, half:DC, c:c + n],
                xT_hi[:, half:DC, c:c + n]).then_inc(xT_lo_ready, 1)

            for i in range(DC):
                dve.wait_ge(wgc_hi_ready, i + 1)
                low(wgc_lo[:, i], wgc_raw[:, i], wgc_hi[:, i]).then_inc(wgc_lo_ready, 1)
                if i == half:
                    q_low(0, 0, 0)
            q_low(0, 0, 1)
            for i in range(EC):
                wmT_low(i)
            c, n = UNITS[1]
            dve.wait_ge(xT_hi_ready, 2)
            low(xT_lo[:, :, c:c + n], xT_raw[:, :, c:c + n], xT_hi[:, :, c:c + n]).then_inc(xT_lo_ready, 1)
            wga_low(0)
            for i in range(half):
                wgx_low(i)
            maximum(0, 0)
            wga_low(1)
            q_low(0, 1, 0)
            for i in range(half, DC):
                wgx_low(i)

            def group(g, last):
                for b in range(GROUP):
                    if b >= 3:
                        gate_context(g, b - 3)
                    if b >= 1:
                        amT_low(g, b - 1)
                    if b > 0:
                        maximum(g, b)
                    if b >= 3:
                        fuse(g, b - 3)
                    shares(g, b)
                    pT_low(g, b)
                    if b == 0:
                        q_low(g, 1, 1)
                    if b in (1, 2):
                        q_low(g, 2, b - 1)
                    if b >= 2:
                        add_bias(g, b - 2)
                    if b >= 3:
                        norm(g, b - 3)
                amT_low(g, GROUP - 1)
                gate_context(g, TILES - 2)
                fuse(g, TILES - 2)
                if last:
                    for cols in HALVES:
                        add_bias(g, TILES - 1, cols)
                    for i, cols in enumerate(HALVES):
                        gate_context(g, TILES - 1, cols, i, late_ps[i])
                    for i, cols in enumerate(HALVES):
                        fuse(g, TILES - 1, cols, i)
                    norm(g, TILES - 2)
                    for cols in HALVES:
                        norm(g, TILES - 1, cols)
                else:
                    q_low(g + 1, 0, 0)
                    add_bias(g, TILES - 1)
                    norm(g, TILES - 2)
                    gate_context(g, TILES - 1)
                    q_low(g + 1, 0, 1)
                    fuse(g, TILES - 1)
                    maximum(g + 1, 0)
                    q_low(g + 1, 1, 0)
                    norm(g, TILES - 1)

            with dve.Fori(0, GROUPS - 1) as g:
                group(g, False)
            group(GROUPS - 1, True)

        @block.gpsimd
        def _(pool):
            def low(out, in_, high):
                return pool.tensor_tensor(out, in_, high.bitcast(F32), ALU.subtract)

            def split_xT(g, unit):
                c, n = UNITS[unit]
                pool.wait_ge(xT_hi_ready, len(UNITS) * g + unit + 1)
                low(xT_lo[:, :, c:c + n], xT_raw[:, :, c:c + n], xT_hi[:, :, c:c + n]).then_inc(xT_lo_ready, 1)

            def split_memT(g, b):
                pool.wait_ge(memT_hi_ready, GROUP * g + b + 1)
                low(memT_lo[:, b % 2], memT_raw[:, b % 2], memT_hi[:, b % 2]).then_inc(memT_lo_ready, 1)

            def split_mem(g, b):
                pool.wait_ge(mem_hi_ready, GROUP * g + b + 1)
                low(mem_lo[:, b % 2], mem_raw[:, b % 2], mem_hi[:, b % 2]).then_inc(mem_lo_ready, 1)

            def inverse_rms(g, t):
                s = slice(t % 2, t % 2 + 1)
                pool.wait_ge(meansq_ready, TILES * g + t + 1)
                pool.tensor_tensor(guarded[:, s], meansq[:, s], eps[:], ALU.add).then_inc(guarded_ready, 1)
                pool.wait_ge(guarded_ready, TILES * g + t + 1)
                pool.tensor_tensor(rstd[:, s], guarded[:, s], minus_half[:], ALU.pow).then_inc(rstd_ready, 1)

            pool.memset(ident[:], 0.0).then_inc(blank_ready, 1)
            pool.wait_ge(blank_ready, 1)
            pool.affine_select(out=ident[:], in_=ident[:], compare_op=ALU.not_equal, fill=1.0, base=0,
                               pattern=[[-1, P]], channel_multiplier=1).then_inc(ident_ready, 1)
            pool.wait_ge(constants_ready, 2)
            split_memT(0, 0)
            split_mem(0, 0)
            pool.wait_ge(xT_lo_ready, 2)
            split_xT(0, 2)

            def group(g, last):
                for b in range(GROUP):
                    ahead = not last or b + 1 < GROUP
                    after = (g, b + 1) if b + 1 < GROUP else (g + 1, 0)
                    if ahead:
                        split_memT(*after)
                    if b >= 3:
                        inverse_rms(g, b - 3)
                    if ahead:
                        split_mem(*after)
                    if not last and b in SPLIT_AT:
                        split_xT(g + 1, SPLIT_AT.index(b))
                inverse_rms(g, TILES - 2)
                if not last:
                    inverse_rms(g, TILES - 1)

            with pool.Fori(0, GROUPS - 1) as g:
                group(g, False)
            group(GROUPS - 1, True)
            a, b = slice(2, 3), slice(3, 4)
            n = TILES * GROUPS
            pool.wait_ge(meansq_ready, n)
            pool.tensor_tensor(guarded[:, a], meansq[:, a], eps[:], ALU.add).then_inc(guarded_ready, 1)
            pool.wait_ge(guarded_ready, n)
            pool.wait_ge(meansq_ready, n + 1)
            pool.tensor_tensor(guarded[:, b], guarded[:, a], meansq[:, b], ALU.add).then_inc(guarded_ready, 1)
            pool.wait_ge(guarded_ready, n + 1)
            pool.tensor_tensor(rstd[:, LAST_SLOT:LAST_SLOT + 1], guarded[:, b], minus_half[:], ALU.pow).then_inc(rstd_ready, 1)


def kernel(x, ctx_1024, L0_xattn_W_mem, L0_xattn_W_gate, L0_xattn_b_gate, L0_xattn_norm_w):
    import numpy as np
    import concourse.bacc as bacc
    from concourse.bass_utils import run_bass_kernel_spmd

    x, memory, w_mem, w_gate, b_gate, norm_w = (
        np.asarray(a) for a in (x, ctx_1024, L0_xattn_W_mem, L0_xattn_W_gate, L0_xattn_b_gate, L0_xattn_norm_w))

    def chunked(a):
        *lead, rows, n = a.shape
        return np.ascontiguousarray(np.swapaxes(a.reshape(*lead, rows // P, P, n), -3, -2))

    def padded(a, axis, size):
        width = [(0, 0)] * a.ndim
        width[axis] = (0, size - a.shape[axis])
        return np.pad(a, width)

    arrays = {
        "x": np.ascontiguousarray(x.reshape(GROUPS * TILES, P, D)),
        "xT": chunked(np.swapaxes(x.reshape(GROUPS, COLS, D), 1, 2)),
        "mem": chunked(padded(memory, 1, KPAD)),
        "memT": chunked(padded(np.swapaxes(memory, 1, 2), 2, KEVEN)),
        "wm": chunked(w_mem),
        "wgT": chunked(w_gate.T),
        "b": np.ascontiguousarray(b_gate),
        "nw": np.ascontiguousarray(norm_w),
    }
    nc = bacc.Bacc("TRN2", target_bir_lowering=False, num_devices=1)
    args = [nc.dram_tensor(f"in_{n}", a.shape, F32, kind="ExternalInput").ap() for n, a in arrays.items()]
    out = nc.dram_tensor("out", (GROUPS * TILES, P, D), F32, kind="ExternalOutput").ap()
    build_gated_cross_attention(nc, *args, out)
    r = run_bass_kernel_spmd(nc, [{f"in_{n}": a for n, a in arrays.items()}], core_ids=[0])
    return r.results[0]["out"].reshape(BATCHES, ROWS, D)
```
